# Optimizing a Trainium2 kernel written in Bass

```python
import numpy as np
import jax
import jax.numpy as jnp

def _softmax(x, axis=-1):
    return jax.nn.softmax(x, axis=axis)

def _gelu(x):
    return jax.nn.gelu(x, approximate=True)

def _silu(x):
    return jax.nn.silu(x)

def _sigmoid(x):
    return jax.nn.sigmoid(x)

def _layernorm(x, axis=-1, eps=1e-05):
    m = jnp.mean(x, axis=axis, keepdims=True)
    v = jnp.var(x, axis=axis, keepdims=True)
    return (x - m) / jnp.sqrt(v + eps)

def _scatter_add(tgt, idx, src, axis=0):
    return tgt.at[idx].add(src)

def _segment_sum(src, seg, n):
    return jax.ops.segment_sum(src, seg, n)
kernel_name = 'mk_flamingo_gated_d1_seqx_r4_583c89'

def setup_inputs(seed: int=0):
    np.random.seed(seed)
    _w = jnp.asarray

    def _rec_inputs():
        import jax
        import jax.numpy as jnp
        _rk = jax.random.key(seed)
        x = -0.0003929 + 0.9999 * jax.random.normal(jax.random.fold_in(_rk, 1), (16, 128, 1024), jnp.float32)
        _lenS = 128 - jax.random.randint(jax.random.fold_in(_rk, 7), (16,), 0, max(1, 128 // 4) + 1, jnp.int32)
        _lenS2 = 128 - jax.random.randint(jax.random.fold_in(_rk, 8), (16,), 0, max(1, 128 // 4) + 1, jnp.int32)
        _ctx_4096P = jax.random.normal(jax.random.fold_in(_rk, 11), (16, 16, 1024), jnp.float32)
        _ctx_4096c = jax.random.dirichlet(jax.random.fold_in(_rk, 511), 0.3 * jnp.ones((16,), jnp.float32), (16, 128))
        _ctx_4096t = jnp.einsum('bsk,bkd->bsd', _ctx_4096c, _ctx_4096P)
        _ctx_4096t = _ctx_4096t * jax.lax.rsqrt(jnp.mean(jnp.square(_ctx_4096t)) + 1e-12) * 0.953939
        ctx_4096 = 2.81802e-05 + 1.00001 * (_ctx_4096t + 0.3 * jax.random.normal(jax.random.fold_in(_rk, 611), (16, 128, 1024), jnp.float32))
        _g = jax.random.normal(jax.random.fold_in(_rk, 9001), (2, 1), jnp.float32)
        _g = jnp.sign(_g) * jnp.maximum(jnp.abs(_g), 1.0) + (_g == 0) * 1.0
        g_xattn = _g[0]
        g_ffn = _g[1]
        return (x, ctx_4096, g_xattn, g_ffn)
    x, ctx_4096, g_xattn, g_ffn = _rec_inputs()

    def _L0_xattn_setup():
        import jax, jax.numpy as jnp
        import numpy as np
        DIM = 128
        HEADS = 8
        DIM_HEAD = 64
        HIDDEN = HEADS * DIM_HEAD
        SCALE = DIM_HEAD ** (-0.5)
        key = jax.random.key(seed)
        ks = jax.random.split(key, 9)
        b, n = (8, 1024)
        std = 1.0 / np.sqrt(DIM)
        return {'q': jax.random.normal(ks[0], (b, DIM, n), jnp.float32), 'k': jax.random.normal(ks[1], (b, DIM, n), jnp.float32), 'v': jax.random.normal(ks[2], (b, DIM, n), jnp.float32), 'Wq': jax.random.normal(ks[3], (HIDDEN, DIM), jnp.float32) * std, 'Wk': jax.random.normal(ks[4], (HIDDEN, DIM), jnp.float32) * std, 'Wv': jax.random.normal(ks[5], (HIDDEN, DIM), jnp.float32) * std, 'Wo': jax.random.normal(ks[6], (DIM, HIDDEN), jnp.float32) * (1.0 / np.sqrt(HIDDEN)), 'bo': jax.random.normal(ks[7], (DIM,), jnp.float32) * 0.01, 'g': jnp.ones((1, DIM, 1), jnp.float32)}
    _L0_xattn_all = _L0_xattn_setup()
    _L0_xattn_in = {k: v for k, v in _L0_xattn_all.items() if k in ('Wq', 'Wk', 'Wv', 'Wo', 'bo', 'g')}
    del _L0_xattn_all

    def _L0_ffn_setup():
        import jax, jax.numpy as jnp
        import numpy as np
        BATCH, SEQ, D = (2, 512, 1024)
        K, TOPK, RANK = (64, 16, 16)
        ALPHA = 32.0
        SCALING = ALPHA / RANK
        key = jax.random.key(seed)
        k1, k2, k3, k4 = jax.random.split(key, 4)
        x = jax.random.normal(k1, (BATCH, SEQ, D), dtype=jnp.float32)
        A = jax.random.normal(k2, (K, RANK, D), dtype=jnp.float32) * 0.02
        B = jax.random.normal(k3, (K, D, RANK), dtype=jnp.float32) * 0.02
        Wr = jax.random.normal(k4, (K, D), dtype=jnp.float32) * 0.02
        return {'x': x, 'A': A, 'B': B, 'Wr': Wr}
    _L0_ffn_all = _L0_ffn_setup()
    _L0_ffn_in = {k: v for k, v in _L0_ffn_all.items() if k in ('A', 'B', 'Wr')}
    del _L0_ffn_all
    return {'x': x, 'ctx_4096': ctx_4096, 'g_xattn': g_xattn, 'g_ffn': g_ffn, 'L0_xattn_Wq': _L0_xattn_in['Wq'], 'L0_xattn_Wk': _L0_xattn_in['Wk'], 'L0_xattn_Wv': _L0_xattn_in['Wv'], 'L0_xattn_Wo': _L0_xattn_in['Wo'], 'L0_xattn_bo': _L0_xattn_in['bo'], 'L0_xattn_g': _L0_xattn_in['g'], 'L0_ffn_A': _L0_ffn_in['A'], 'L0_ffn_B': _L0_ffn_in['B'], 'L0_ffn_Wr': _L0_ffn_in['Wr']}

def reference(x, ctx_4096, g_xattn, g_ffn, L0_xattn_Wq, L0_xattn_Wk, L0_xattn_Wv, L0_xattn_Wo, L0_xattn_bo, L0_xattn_g, L0_ffn_A, L0_ffn_B, L0_ffn_Wr):
    import jax
    import jax.numpy as jnp

    def _L0_xattn_ref(q, k, v, Wq, Wk, Wv, Wo, bo, g):
        import jax, jax.numpy as jnp
        import numpy as np
        DIM = 128
        HEADS = 8
        DIM_HEAD = 64
        HIDDEN = HEADS * DIM_HEAD
        SCALE = DIM_HEAD ** (-0.5)
        b = q.shape[0]
        qh = jnp.einsum('bcn,oc->bon', q, Wq).reshape(b, HEADS, DIM_HEAD, -1)
        kh = jnp.einsum('bcn,oc->bon', k, Wk).reshape(b, HEADS, DIM_HEAD, -1)
        vh = jnp.einsum('bcn,oc->bon', v, Wv).reshape(b, HEADS, DIM_HEAD, -1)
        qh = jax.nn.softmax(qh, axis=-2) * SCALE
        kh = jax.nn.softmax(kh, axis=-1)
        context = jnp.einsum('bhdn,bhen->bhde', kh, vh)
        out = jnp.einsum('bhde,bhdn->bhen', context, qh)
        out = out.reshape(b, HIDDEN, -1)
        out = jnp.einsum('bcn,oc->bon', out, Wo) + bo[None, :, None]
        norm = jnp.maximum(jnp.sqrt(jnp.sum(out * out, axis=1, keepdims=True)), 1e-12)
        return out / norm * g * np.sqrt(DIM)

    def _L0_ffn_ref(x, A, B, Wr):
        import jax, jax.numpy as jnp
        import numpy as np
        BATCH, SEQ, D = (2, 512, 1024)
        K, TOPK, RANK = (64, 16, 16)
        ALPHA = 32.0
        SCALING = ALPHA / RANK
        prefix = x.shape[:-1]
        xf = x.reshape(-1, x.shape[-1])
        N = xf.shape[0]
        scores = xf @ Wr.T
        top_vals, top_idx = jax.lax.top_k(scores, TOPK)
        gates = jax.nn.softmax(top_vals, axis=-1)
        G = jnp.zeros((N, K), xf.dtype).at[jnp.arange(N)[:, None], top_idx].set(gates)
        h = jnp.einsum('nd,krd->nkr', xf, A)
        out = jnp.einsum('nkr,kdr->nd', h * G[:, :, None], B)
        return (out * SCALING).reshape(*prefix, -1)
    x = x + jnp.tanh(g_xattn[0]) * _L0_xattn_ref(_layernorm(x, axis=-1), ctx_4096, ctx_4096, L0_xattn_Wq, L0_xattn_Wk, L0_xattn_Wv, L0_xattn_Wo, L0_xattn_bo, L0_xattn_g)
    x = x + jnp.tanh(g_ffn[0]) * _L0_ffn_ref(_layernorm(x, axis=-1), L0_ffn_A, L0_ffn_B, L0_ffn_Wr)
    return x

_drawn_inputs = setup_inputs


def setup_inputs(seed=0):
    import zlib

    import numpy as np

    out = dict(_drawn_inputs(seed))
    spreads = {'L0_xattn_g': (1.0, 0.2)}
    factors = {}
    for name, (base, spread) in spreads.items():
        noise = np.random.default_rng([zlib.crc32(name.encode()), seed]).standard_normal(out[name].shape)
        drawn = base * np.exp(spread * noise) if base else spread * noise
        out[name] = jnp.asarray(drawn.astype(out[name].dtype))
    for name, factor in factors.items():
        out[name] = (out[name] * factor).astype(out[name].dtype)
    return out
```

```python
import concourse.bass as bass
from concourse import mybir
from contextlib import ExitStack
import math


def flamingo_layer(nc, x, ctx, g_xattn, g_ffn, Wq, Wk, Wv, Wo, bo, g, A, B, Wr, x2_dram, out):
    f32 = mybir.dt.float32
    f32r = mybir.dt.float32r
    i32 = mybir.dt.int32
    ALU = mybir.AluOpType
    ACT = mybir.ActivationFunctionType
    AX = mybir.AxisListType

    NB, C, N = x.shape
    HD = Wq.shape[0]
    DH = 64
    P = 128
    H = HD // DH
    CH = HD // P
    BK = N // P
    HF = N // 512
    E, R = A.shape[0], A.shape[1]
    KR = E * R
    LN_EPS = 1e-5
    MIN_SS = 1e-24
    MAGIC = 1597463007
    NEWTON = 3
    NCH = 2 + 3 * NEWTON
    NEG = -3.0e38

    def started(b):
        return not (isinstance(b, int) and b == 0)

    def wait_apart(eng, turns, *waits):
        for sem, value in waits:
            eng.wait_ge(sem, value)
        eng.sem_inc(turns, 1)

    def rsqrt_chain(dve, y, t, s, sem, base):
        nc.vector.tensor_scalar(t.bitcast(i32), s.bitcast(i32), 1, None,
                                ALU.logical_shift_right).then_inc(sem, 1)
        dve.wait_ge(sem, base + 1)
        nc.vector.tensor_scalar(y.bitcast(i32), t.bitcast(i32), -1.0, float(MAGIC),
                                ALU.mult, ALU.add).then_inc(sem, 1)
        for k in range(NEWTON):
            dve.wait_ge(sem, base + 2 + 3 * k)
            nc.vector.tensor_tensor(t, y, s, ALU.mult).then_inc(sem, 1)
            dve.wait_ge(sem, base + 3 + 3 * k)
            nc.vector.scalar_tensor_tensor(t, t, -0.5, y, ALU.mult, ALU.mult).then_inc(sem, 1)
            dve.wait_ge(sem, base + 4 + 3 * k)
            nc.vector.scalar_tensor_tensor(y, t, 1.5, y, ALU.add, ALU.mult).then_inc(sem, 1)

    def three_pass(psum, whi, wlo, mhi, mlo, start, stop):
        nc.tensor.matmul(psum, whi, mhi, start=start, stop=False)
        nc.tensor.matmul(psum, wlo, mhi, start=False, stop=False)
        return nc.tensor.matmul(psum, whi, mlo, start=False, stop=stop)

    outer = ExitStack()
    with outer:
        def const(name, shape, dt=f32):
            return outer.enter_context(nc.sbuf_tensor(name, shape, dt))

        def osem(name):
            return outer.enter_context(nc.semaphore(name))

        ident = const("ident", [P, P])
        ident_r = const("ident_r", [P, P], f32r)
        gates = const("gates", [P, 2])
        ps = outer.enter_context(nc.psum_tensor("ps", [P, 8, 512], f32))
        psK = ps[:, 0:2, :]
        psQ = ps[:, 2:4, :]
        psT = ps[:, 4:6, :]
        psX = ps[:, 6:8, :]

        with ExitStack() as ph:
            def sb(name, shape, dt=f32):
                return ph.enter_context(nc.sbuf_tensor(name, shape, dt))

            def sem(name):
                return ph.enter_context(nc.semaphore(name))

            wstage = sb("wstage", [P, 4, CH, P])
            wk = [sb("wk_hi", [P, HD], f32r), sb("wk_lo", [P, HD], f32r)]
            wq = [sb("wq_hi", [P, HD], f32r), sb("wq_lo", [P, HD], f32r)]
            woT = sb("woT", [P, CH, P])
            wvo = [sb("wvo_hi", [P, CH, 2 * P], f32r), sb("wvo_lo", [P, CH, 2 * P], f32r)]
            g_raw = sb("g_raw", [P, 4])
            gcol = sb("gcol", [P, 1])
            ones = sb("ones", [P, 1])
            ctx_in = sb("ctx_in", [P, N])
            x_in = sb("x_in", [P, N])
            x_res = sb("x_res", [P, N])
            cx = [sb("ctx_hi", [P, N], f32r), sb("ctx_lo", [P, N], f32r)]
            xn = sb("xn", [P, N])
            xs = [sb("xn_hi", [P, N], f32r), sb("xn_lo", [P, N], f32r)]
            cT = [sb("ctxT_hi", [P, BK, C], f32r), sb("ctxT_lo", [P, BK, C], f32r)]
            ek = sb("ek", [P, 2, N])
            ekT = [sb("ekT_hi", [P, BK, HD], f32r), sb("ekT_lo", [P, BK, HD], f32r)]
            kmax = sb("kmax", [P, CH])
            ksum = sb("ksum", [P, CH])
            krec = sb("krec", [P, CH])
            qe = sb("qe", [P, 2, 2 * HD])
            qmax = sb("qmax", [P, 2, 2 * H], f32r)
            qsum = sb("qsum", [P, 2, 2 * H])
            qrec = sb("qrec", [P, 2, 2 * H])
            qT = [sb("qT_hi", [P, CH, N], f32r), sb("qT_lo", [P, CH, N], f32r)]
            kc = [sb("kc_hi", [P, HD], f32r), sb("kc_lo", [P, HD], f32r)]
            mt = sb("mt", [P, CH, P])
            mts = [sb("mt_hi", [P, CH, P], f32r), sb("mt_lo", [P, CH, P], f32r)]
            osb = sb("osb", [P, N])
            osq = sb("osq", [P, N])
            usb = sb("usb", [P, N])
            x2 = sb("x2", [P, N])
            bn = sb("bn", [P, HF, 6])
            mv = sb("mv", [P, 2])
            s9 = sb("s9", [P, BK + 1])
            y9 = sb("y9", [P, BK + 1])
            t9 = sb("t9", [P, BK + 1])
            nbias = sb("nbias", [P, 1])
            rn = [sb("rn_hi", [P, BK], f32r), sb("rn_lo", [P, BK], f32r)]

            pool_turns, dve_turns = sem("pool_turns"), sem("dve_turns")
            w_loaded, id_ready, ones_ready = sem("w_loaded"), sem("id_ready"), sem("ones_ready")
            wT_done, w_hi, w_lo = sem("wT_done"), sem("w_hi"), sem("w_lo")
            fold_done, fold_hi, fold_lo = sem("fold_done"), sem("fold_hi"), sem("fold_lo")
            tanh_done, gcol_done = sem("tanh_done"), sem("gcol_done")
            ctx_loaded, x_loaded, xres_loaded, x2_stored = (
                sem("ctx_loaded"), sem("x_loaded"), sem("xres_loaded"), sem("x2_stored"))
            ctx_split, xn_split = sem("ctx_split"), sem("xn_split")
            stats_step, newton_step, nbias_done, xn_done = (
                sem("stats_step"), sem("newton_step"), sem("nbias_done"), sem("xn_done"))
            k_mm, k_max, k_exp, k_T, k_hi, k_lo, k_rec = (
                sem("k_mm"), sem("k_max"), sem("k_exp"), sem("k_T"), sem("k_hi"), sem("k_lo"),
                sem("k_rec"))
            q_mm, q_max, q_shift, q_exp, q_sum, q_rec, q_norm, q_T, q_hi, q_lo = (
                sem("q_mm"), sem("q_max"), sem("q_shift"), sem("q_exp"), sem("q_sum"),
                sem("q_rec"), sem("q_norm"), sem("q_T"), sem("q_hi"), sem("q_lo"))
            c_T, c_hi, c_lo = sem("c_T"), sem("c_hi"), sem("c_lo")
            kc_mm, kc_hi, kc_lo = sem("kc_mm"), sem("kc_hi"), sem("kc_lo")
            m_mm, m_scaled, m_hi, m_lo = sem("m_mm"), sem("m_scaled"), sem("m_hi"), sem("m_lo")
            o_mm, o_out, ss_mm, ss_read, rn_done, rn_mm, u_done, x2_done = (
                sem("o_mm"), sem("o_out"), sem("ss_mm"), sem("ss_read"), sem("rn_done"),
                sem("rn_mm"), sem("u_done"), sem("x2_done"))

            def run(eng, body, between=None):
                body(0, True, False, True)
                with eng.Fori(1, NB - 1) as b:
                    body(b, True, True, True)
                body(NB - 1, True, True, False)
                body(NB, False, True, False)

            block = ph.enter_context(nc.Block())

            @block.sync
            def _(sp):
                def load(dst, src, b, s):
                    sp.dma_start(dst, src[bass.ds(b, 1)].rearrange("o p n -> (o p) n")).then_inc(s, 16)

                load(ctx_in[:, :], ctx, 0, ctx_loaded)
                load(x_in[:, :], x, 0, x_loaded)
                load(x_res[:, :], x, 0, xres_loaded)
                xn_first = 1
                sp.wait_ge(xn_done, xn_first)
                load(x_in[:, :], x, 1, x_loaded)

                def body(b, head, tail, nxt):
                    if nxt:
                        sp.wait_ge(c_T, 2 * b + 2)
                        load(ctx_in[:, :], ctx, b + 1, ctx_loaded)
                        sp.wait_ge(xn_done, b + 2)
                        if not (isinstance(b, int) and b == NB - 2):
                            load(x_in[:, :], x, b + 2, x_loaded)
                    if tail:
                        sp.wait_ge(x2_done, b)
                        sp.dma_start(x2_dram[bass.ds(b - 1, 1)].rearrange("o p n -> (o p) n"),
                                     x2[:, :]).then_inc(x2_stored, 16)
                        if head:
                            load(x_res[:, :], x, b, xres_loaded)

                body(0, True, False, True)
                with sp.Fori(1, NB - 2) as b:
                    body(b, True, True, True)
                body(NB - 2, True, True, True)
                body(NB - 1, True, True, False)
                body(NB, False, True, False)
                sp.wait_ge(x2_stored, 16 * NB)

            @block.gpsimd
            def _(pool):
                nc.gpsimd.memset(ident[:, :], 0.0).then_inc(id_ready, 1)
                pool.wait_ge(id_ready, 1)
                nc.gpsimd.affine_select(out=ident[:, :], in_=ident[:, :], compare_op=ALU.not_equal,
                                        fill=1.0, base=0, pattern=[[-1, P]],
                                        channel_multiplier=1).then_inc(id_ready, 1)
                pool.wait_ge(id_ready, 2)
                nc.gpsimd.tensor_scalar(ident_r[:, :], ident[:, :], 1.0, 0.0, ALU.mult,
                                        ALU.add).then_inc(id_ready, 1)
                nc.gpsimd.memset(ones[:, :], 1.0).then_inc(ones_ready, 1)

                def split(parts, src, s, value):
                    nc.gpsimd.tensor_scalar(parts[0], src, 1.0, 0.0, ALU.mult, ALU.add).then_inc(s, 1)
                    pool.wait_ge(s, value)
                    nc.gpsimd.tensor_tensor(parts[1], src, parts[0].bitcast(f32),
                                            ALU.subtract).then_inc(s, 1)

                def split_ctx(b):
                    split([cx[0][:, :], cx[1][:, :]], ctx_in[:, :], ctx_split, 2 * b + 1)

                def split_xn(b):
                    split([xs[0][:, :], xs[1][:, :]], xn[:, :], xn_split, 2 * b + 1)

                def normalise(b, p):
                    pool.wait_ge(q_rec, 4 * b + p + 1)
                    v = qe[:, p % 2, :].rearrange("p (h d) -> p h d", d=DH)
                    w = qrec[:, p % 2, :].unsqueeze(2).broadcast_to([P, 2 * H, DH])
                    nc.gpsimd.tensor_tensor(v, v, w, ALU.mult).then_inc(q_norm, 1)

                pool.wait_ge(ctx_loaded, 16)
                split_ctx(0)
                pool.wait_ge(xn_done, 1)
                split_xn(0)

                def body(b, head, tail, nxt):
                    if tail:
                        pool.wait_ge(m_hi, b)
                        nc.gpsimd.tensor_tensor(mts[1][:, :, :], mt[:, :, :], mts[0][:, :, :].bitcast(f32),
                                                ALU.subtract).then_inc(m_lo, 1)
                    if head:
                        normalise(b, 0)
                        normalise(b, 1)
                    if tail:
                        pool.wait_ge(xres_loaded, 16 * b)
                        if not (isinstance(b, int) and b == 1):
                            pool.wait_ge(x2_stored, 16 * (b - 1))
                        pool.wait_ge(u_done, 2 * b)
                        nc.gpsimd.tensor_tensor(x2[:, :], usb[:, :], x_res[:, :],
                                                ALU.add).then_inc(x2_done, 1)
                    if head:
                        normalise(b, 2)
                    if nxt:
                        wait_apart(pool, pool_turns, (k_mm, 4 * b + 4), (ctx_loaded, 16 * (b + 2)))
                        split_ctx(b + 1)
                    if head:
                        normalise(b, 3)
                    if nxt:
                        wait_apart(pool, pool_turns, (q_mm, 4 * b + 4), (xn_done, b + 2))
                        split_xn(b + 1)

                body(0, True, False, True)
                body(1, True, True, True)
                with pool.Fori(2, NB - 1) as b:
                    body(b, True, True, True)
                body(NB - 1, True, True, False)
                body(NB, False, True, False)

            @block.scalar
            def _(act):
                act.dma_start(wstage[:, 0, :, :], Wk.rearrange("(j p) c -> p j c", p=P)).then_inc(w_loaded, 16)
                act.dma_start(wstage[:, 1, :, :], Wq.rearrange("(j p) c -> p j c", p=P)).then_inc(w_loaded, 16)
                act.dma_start(wstage[:, 2, :, :], Wv.rearrange("(j p) c -> p j c", p=P)).then_inc(w_loaded, 16)
                act.dma_start(wstage[:, 3, :, :], Wo.rearrange("o (j c) -> o j c", c=P)).then_inc(w_loaded, 16)
                act.dma_start(g_raw[:, 0:1], g_xattn.rearrange("(a n) -> a n", a=1).broadcast_to([P, 1])).then_inc(w_loaded, 16)
                act.dma_start(g_raw[:, 1:2], g_ffn.rearrange("(a n) -> a n", a=1).broadcast_to([P, 1])).then_inc(w_loaded, 16)
                act.dma_start(g_raw[:, 2:3], g[0]).then_inc(w_loaded, 16)
                act.dma_start(g_raw[:, 3:4], bo.rearrange("(p a) -> p a", a=1)).then_inc(w_loaded, 16)
                act.wait_ge(w_loaded, 128)
                nc.scalar.activation(gates[:, :], g_raw[:, 0:2], ACT.Tanh).then_inc(tanh_done, 1)
                bo_col = g_raw[:, 3:4]

                act.wait_ge(wT_done, 1)
                nc.scalar.activation(wk[0][:, :], psT[:, 0, :], ACT.Copy).then_inc(w_hi, 1)
                act.wait_ge(wT_done, 2)
                nc.scalar.activation(wq[0][:, :], psT[:, 1, :], ACT.Copy).then_inc(w_hi, 1)
                act.wait_ge(wT_done, 3)
                nc.scalar.activation(woT[:, :, :].rearrange("p a b -> p (a b)"), psK[:, 0, :],
                                     ACT.Copy).then_inc(w_hi, 1)
                act.wait_ge(fold_done, 1)
                for par in range(2):
                    nc.scalar.activation(wvo[0][:, :, par * P:par * P + P],
                                         psX[:, par, :].rearrange("p (j o) -> p j o", o=P),
                                         ACT.Copy, scale=DH ** -0.5).then_inc(fold_hi, 1)

                def norm_x(b):
                    act.wait_ge(nbias_done, b + 1)
                    nc.scalar.activation(xn[:, :], x_in[:, :], ACT.Identity, bias=nbias[:, 0:1],
                                         scale=y9[:, BK:BK + 1]).then_inc(xn_done, 1)

                norm_x(0)

                def exp_k(b, j):
                    act.wait_ge(k_max, 4 * b + j + 1)
                    if j == 0 and not isinstance(b, int):
                        act.wait_ge(k_rec, b)
                    if j == 0 and isinstance(b, int) and b > 0:
                        act.wait_ge(k_rec, b)
                    if j >= 2:
                        act.wait_ge(k_T, 8 * b + 2 * (j - 2) + 2)
                    elif started(b):
                        act.wait_ge(k_T, 8 * b - 8 + 2 * (j + 2) + 2)
                    nc.scalar.activation(ek[:, j % 2, :].rearrange("p (a n) -> p a n", a=HF), psK,
                                         ACT.Exp, bias=kmax[:, j:j + 1],
                                         accum_out=ksum[:, j:j + 1]).then_inc(k_exp, 1)

                def exp_q(b, p):
                    act.wait_ge(q_shift, 4 * b + p + 1)
                    if p >= 2:
                        act.wait_ge(q_T, 8 * b + 2 * (p - 2) + 2)
                    elif started(b):
                        act.wait_ge(q_T, 8 * b - 8 + 2 * (p + 2) + 2)
                    nc.scalar.activation(qe[:, p % 2, :].rearrange("p (a n) -> p a n", a=2), psQ,
                                         ACT.Exp).then_inc(q_exp, 1)

                def hi_q(b, p):
                    for h in range(2):
                        act.wait_ge(q_T, 8 * b + 2 * p + h + 1)
                        nb = 2 * p + h
                        nc.scalar.activation(qT[0][:, :, nb * P:nb * P + P],
                                             psT[:, h, :].rearrange("p (j n) -> p j n", n=P),
                                             ACT.Copy).then_inc(q_hi, 1)

                def hi_k(b, j):
                    for h in range(2):
                        act.wait_ge(k_T, 8 * b + 2 * j + h + 1)
                        nc.scalar.activation(ekT[0][:, 4 * h:4 * h + 4, j * P:j * P + P],
                                             psT[:, h, :].rearrange("p (n d) -> p n d", d=P),
                                             ACT.Copy).then_inc(k_hi, 1)

                def out_o(b, h):
                    act.wait_ge(o_mm, 2 * b + h + 1)
                    v = slice(512 * h, 512 * h + 512)
                    nc.scalar.activation(osb[:, v], psX[:, h, :], ACT.Identity, bias=bo_col)
                    nc.scalar.activation(osq[:, v], psX[:, h, :], ACT.Square, bias=bo_col).then_inc(o_out, 1)

                def body(b, head, tail, nxt):
                    if head:
                        exp_k(b, 0)
                    if tail:
                        hi_q(b - 1, 3)
                        act.wait_ge(kc_mm, b)
                        nc.scalar.activation(kc[0][:, :], psX[:, 0, :], ACT.Copy).then_inc(kc_hi, 1)
                    if head:
                        for h in range(2):
                            act.wait_ge(c_T, 2 * b + h + 1)
                            nc.scalar.activation(cT[0][:, 4 * h:4 * h + 4, :],
                                                 psT[:, h, :].rearrange("p (n c) -> p n c", c=P),
                                                 ACT.Copy).then_inc(c_hi, 1)
                        hi_k(b, 0)
                    if tail:
                        act.wait_ge(m_scaled, 2 * b)
                        nc.scalar.activation(mts[0][:, :, :], mt[:, :, :], ACT.Copy).then_inc(m_hi, 1)
                    if head:
                        exp_q(b, 0)
                        exp_k(b, 1)
                    if tail:
                        out_o(b - 1, 0)
                    if head:
                        hi_k(b, 1)
                    if tail:
                        out_o(b - 1, 1)
                    if head:
                        exp_q(b, 1)
                        exp_k(b, 2)
                        hi_q(b, 0)
                        hi_k(b, 2)
                    if nxt:
                        act.wait_ge(xn_split, 2 * b + 2)
                        norm_x(b + 1)
                    if head:
                        exp_k(b, 3)
                        exp_q(b, 2)
                        hi_q(b, 1)
                        hi_k(b, 3)
                        exp_q(b, 3)
                        hi_q(b, 2)

                run(act, body)

            @block.vector
            def _(dve):
                nc.vector.memset(s9[:, :], 1.0).then_inc(stats_step, 1)
                dve.wait_ge(tanh_done, 1)
                nc.vector.scalar_tensor_tensor(gcol[:, :], g_raw[:, 2:3], math.sqrt(C), gates[:, 0:1],
                                               ALU.mult, ALU.mult).then_inc(gcol_done, 1)
                NS = HF + 2

                def stats(b):
                    dve.wait_ge(x_loaded, 16 * (b + 1))
                    for h in range(HF):
                        nc.vector.bn_stats(bn[:, h, :], x_in[:, 512 * h:512 * h + 512]).then_inc(stats_step, 1)
                    wait_apart(dve, dve_turns, (stats_step, 1 + NS * b + HF))
                    nc.vector.bn_aggr(mv[:, :], bn[:, :, :].rearrange("p a b -> p (a b)")).then_inc(stats_step, 1)
                    dve.wait_ge(stats_step, 1 + NS * b + HF + 1)
                    nc.vector.tensor_scalar(s9[:, BK:BK + 1], mv[:, 1:2], LN_EPS, None,
                                            ALU.add).then_inc(stats_step, 1)

                def newton(n, b_stats):
                    if b_stats is not None:
                        dve.wait_ge(stats_step, 1 + NS * (b_stats + 1))
                    rsqrt_chain(dve, y9[:, :], t9[:, :], s9[:, :], newton_step, NCH * n)
                    dve.wait_ge(newton_step, NCH * (n + 1))
                    if b_stats is not None:
                        nc.vector.scalar_tensor_tensor(nbias[:, :], mv[:, 0:1], -1.0, y9[:, BK:BK + 1],
                                                       ALU.mult, ALU.mult).then_inc(nbias_done, 1)

                stats(0)
                newton(0, 0)
                for n, w in enumerate((wk, wq)):
                    dve.wait_ge(w_hi, n + 1)
                    nc.vector.tensor_tensor(w[1][:, :], psT[:, n, :], w[0][:, :].bitcast(f32),
                                            ALU.subtract).then_inc(w_lo, 1)
                for par in range(2):
                    dve.wait_ge(fold_hi, 2)
                    nc.vector.scalar_tensor_tensor(wvo[1][:, :, par * P:par * P + P],
                                                   psX[:, par, :].rearrange("p (j o) -> p j o", o=P), DH ** -0.5,
                                                   wvo[0][:, :, par * P:par * P + P].bitcast(f32),
                                                   ALU.mult, ALU.subtract).then_inc(fold_lo, 1)

                def max_k(b, j):
                    dve.wait_ge(k_mm, 4 * b + j + 1)
                    nc.vector.tensor_reduce(kmax[:, j:j + 1], psK, axis=AX.XY, op=ALU.max,
                                            negate=True).then_inc(k_max, 1)

                def max_q(b, p):
                    dve.wait_ge(q_mm, 4 * b + p + 1)
                    nc.vector.tensor_reduce(qmax[:, p % 2, :], psQ.rearrange("p a (h d) -> p (a h) d", d=DH),
                                            axis=AX.X, op=ALU.max, negate=True).then_inc(q_max, 1)

                def sum_q(b, p):
                    dve.wait_ge(q_exp, 4 * b + p + 1)
                    nc.vector.tensor_reduce(qsum[:, p % 2, :], qe[:, p % 2, :].rearrange("p (h d) -> p h d", d=DH),
                                            axis=AX.X, op=ALU.add).then_inc(q_sum, 1)
                    dve.wait_ge(q_sum, 4 * b + p + 1)
                    nc.vector.reciprocal(qrec[:, p % 2, :], qsum[:, p % 2, :]).then_inc(q_rec, 1)

                def lo_q(b, p):
                    for h in range(2):
                        dve.wait_ge(q_hi, 8 * b + 2 * p + h + 1)
                        nb = 2 * p + h
                        nc.vector.tensor_tensor(qT[1][:, :, nb * P:nb * P + P],
                                                psT[:, h, :].rearrange("p (j n) -> p j n", n=P),
                                                qT[0][:, :, nb * P:nb * P + P].bitcast(f32),
                                                ALU.subtract).then_inc(q_lo, 1)

                def lo_k(b, j):
                    for h in range(2):
                        dve.wait_ge(k_hi, 8 * b + 2 * j + h + 1)
                        nc.vector.tensor_tensor(ekT[1][:, 4 * h:4 * h + 4, j * P:j * P + P],
                                                psT[:, h, :].rearrange("p (n d) -> p n d", d=P),
                                                ekT[0][:, 4 * h:4 * h + 4, j * P:j * P + P].bitcast(f32),
                                                ALU.subtract).then_inc(k_lo, 1)

                def body(b, head, tail, nxt):
                    if head:
                        max_k(b, 0)
                    if tail:
                        lo_q(b - 1, 3)
                        dve.wait_ge(kc_hi, b)
                        nc.vector.tensor_tensor(kc[1][:, :], psX[:, 0, :], kc[0][:, :].bitcast(f32),
                                                ALU.subtract).then_inc(kc_lo, 1)
                    if head:
                        for h in range(2):
                            dve.wait_ge(c_hi, 2 * b + h + 1)
                            nc.vector.tensor_tensor(cT[1][:, 4 * h:4 * h + 4, :],
                                                    psT[:, h, :].rearrange("p (n c) -> p n c", c=P),
                                                    cT[0][:, 4 * h:4 * h + 4, :].bitcast(f32),
                                                    ALU.subtract).then_inc(c_lo, 1)
                        max_q(b, 0)
                    if tail:
                        dve.wait_ge(m_mm, b)
                        dve.wait_ge(k_rec, b)
                        v = psX.rearrange("p a (c w) -> p (a c) w", w=2 * P)
                        for par in range(2):
                            r = slice(DH * par, DH * par + DH)
                            nc.vector.tensor_tensor(mt[r, :, :], v[r, :, par * P:par * P + P],
                                                    krec[r, :].unsqueeze(2).broadcast_to([DH, CH, P]),
                                                    ALU.mult).then_inc(m_scaled, 1)
                    if head:
                        lo_k(b, 0)
                        max_k(b, 1)
                        sum_q(b, 0)
                        max_q(b, 1)
                        lo_k(b, 1)
                        sum_q(b, 1)
                        max_k(b, 2)
                    if nxt:
                        stats(b + 1)
                    if head:
                        lo_q(b, 0)
                    if tail:
                        dve.wait_ge(ss_mm, b)
                        nc.vector.tensor_scalar(s9[:, 0:BK], psX[:, 0, 0:BK], MIN_SS, None,
                                                ALU.max).then_inc(ss_read, 1)
                        dve.wait_ge(ss_read, b)
                    if tail or nxt:
                        newton(b + 1, b + 1 if nxt else None)
                    if tail:
                        nc.vector.tensor_copy(rn[0][:, :], y9[:, 0:BK]).then_inc(rn_done, 1)
                        dve.wait_ge(rn_done, 2 * b - 1)
                        nc.vector.tensor_tensor(rn[1][:, :], y9[:, 0:BK], rn[0][:, :].bitcast(f32),
                                                ALU.subtract).then_inc(rn_done, 1)
                    if head:
                        max_q(b, 2)
                        lo_k(b, 2)
                        max_k(b, 3)
                    if tail:
                        for h in range(2):
                            dve.wait_ge(rn_mm, 2 * b - 2 + h + 1)
                            v = slice(512 * h, 512 * h + 512)
                            nc.vector.scalar_tensor_tensor(usb[:, v], osb[:, v], gcol[:, 0:1], psT[:, h, :],
                                                           ALU.mult, ALU.mult).then_inc(u_done, 1)
                    if head:
                        sum_q(b, 2)
                        lo_q(b, 1)
                        max_q(b, 3)
                        lo_k(b, 3)
                        sum_q(b, 3)
                        dve.wait_ge(k_exp, 4 * b + 4)
                        nc.vector.reciprocal(krec[:, :], ksum[:, :]).then_inc(k_rec, 1)
                        lo_q(b, 2)

                run(dve, body)

            @block.tensor
            def _(pe):
                pe.wait_ge(id_ready, 3)
                pe.wait_ge(w_loaded, 128)
                for n, dst in ((0, psT[:, 0, :]), (1, psT[:, 1, :]), (3, psK[:, 0, :])):
                    for j in range(CH):
                        last = nc.tensor.transpose(dst[:, j * P:j * P + P], wstage[:, n, j, :], ident[:, :])
                    last.then_inc(wT_done, 1)
                pe.wait_ge(w_hi, 3)
                for par in range(2):
                    r = slice(DH * par, DH * par + DH)
                    for j in range(CH):
                        last = nc.tensor.matmul(psX[:, par, j * P:j * P + P], wstage[r, 2, j, :],
                                                woT[r, j, :], start=True, stop=True)
                last.then_inc(fold_done, 1)
                pe.wait_ge(w_lo, 2)
                pe.wait_ge(fold_lo, 2)
                pe.wait_ge(ones_ready, 1)

                def free_T(task, h):
                    kind, b, n = task
                    if kind == "c":
                        pe.wait_ge(c_lo, 2 * b + h + 1)
                    if kind == "k":
                        pe.wait_ge(k_lo, 8 * b + 2 * n + h + 1)
                    if kind == "q":
                        pe.wait_ge(q_lo, 8 * b + 2 * n + h + 1)
                    if kind == "r":
                        pe.wait_ge(u_done, 2 * b + h + 1)

                def mm_k(b, j):
                    if j == 0:
                        pe.wait_ge(ctx_split, 2 * b + 2)
                    if j > 0:
                        pe.wait_ge(k_exp, 4 * b + j)
                    elif started(b):
                        pe.wait_ge(k_exp, 4 * b)
                    for h in range(HF):
                        v = slice(512 * h, 512 * h + 512)
                        w = slice(P * j, P * j + P)
                        last = three_pass(psK[:, h, :], wk[0][:, w], wk[1][:, w], cx[0][:, v], cx[1][:, v],
                                          True, True)
                    last.then_inc(k_mm, 1)

                def mm_q(b, p):
                    if p == 0:
                        pe.wait_ge(xn_split, 2 * b + 2)
                    if p > 0:
                        pe.wait_ge(q_exp, 4 * b + p)
                    elif started(b):
                        pe.wait_ge(q_exp, 4 * b)
                    for h in range(2):
                        w = slice(P * (2 * p + h), P * (2 * p + h) + P)
                        last = three_pass(psQ[:, h, :], xs[0][:, w], xs[1][:, w], wq[0][:, :], wq[1][:, :],
                                          True, True)
                    last.then_inc(q_mm, 1)

                def shift_q(b, p):
                    pe.wait_ge(q_max, 4 * b + p + 1)
                    for h in range(2):
                        m = qmax[:, p % 2, h * H:h * H + H].unsqueeze(2).broadcast_to([P, H, DH])
                        last = nc.tensor.matmul(psQ[:, h, :], ident_r[:, :], m, start=False, stop=True,
                                                skip_group_check=True)
                    last.then_inc(q_shift, 1)

                def tr_c(b, before):
                    for h in range(2):
                        if before:
                            free_T(before, h)
                        for n in range(4):
                            w = (4 * h + n) * P
                            last = nc.tensor.transpose(psT[:, h, n * P:n * P + P], ctx_in[:, w:w + P], ident[:, :])
                        last.then_inc(c_T, 1)

                def tr_k(b, j, before):
                    pe.wait_ge(k_exp, 4 * b + j + 1)
                    for h in range(2):
                        free_T(before, h)
                        for n in range(4):
                            w = (4 * h + n) * P
                            last = nc.tensor.transpose(psT[:, h, n * P:n * P + P], ek[:, j % 2, w:w + P], ident[:, :])
                        last.then_inc(k_T, 1)

                def tr_q(b, p, before):
                    pe.wait_ge(q_norm, 4 * b + p + 1)
                    for h in range(2):
                        free_T(before, h)
                        for j in range(CH):
                            w = h * HD + j * P
                            last = nc.tensor.transpose(psT[:, h, j * P:j * P + P], qe[:, p % 2, w:w + P], ident[:, :])
                        last.then_inc(q_T, 1)

                def context(b):
                    pe.wait_ge(k_lo, 8 * b + 8)
                    pe.wait_ge(c_lo, 2 * b + 2)
                    if started(b):
                        pe.wait_ge(ss_read, b)
                    for n in range(BK):
                        last = three_pass(psX[:, 0, :], cT[0][:, n, :], cT[1][:, n, :], ekT[0][:, n, :],
                                          ekT[1][:, n, :], n == 0, n == BK - 1)
                    last.then_inc(kc_mm, 1)

                def fold(b):
                    pe.wait_ge(kc_lo, b + 1)
                    for j in range(CH):
                        w = slice(P * j, P * j + P)
                        last = three_pass(psX[:, j // 2, (j % 2) * 2 * P:(j % 2) * 2 * P + 2 * P],
                                          kc[0][:, w], kc[1][:, w], wvo[0][:, j, :], wvo[1][:, j, :], True, True)
                    last.then_inc(m_mm, 1)

                def output(b, h):
                    if h == 0:
                        pe.wait_ge(m_lo, b + 1)
                        pe.wait_ge(q_lo, 8 * b + 8)
                    v = slice(512 * h, 512 * h + 512)
                    for j in range(CH):
                        last = three_pass(psX[:, h, :], mts[0][:, j, :], mts[1][:, j, :], qT[0][:, j, v],
                                          qT[1][:, j, v], j == 0, j == CH - 1)
                    last.then_inc(o_mm, 1)

                def square_norms(b):
                    pe.wait_ge(o_out, 2 * b + 2)
                    for n in range(BK):
                        last = nc.tensor.matmul(psX[:, 0, n:n + 1], osq[:, n * P:n * P + P], ones[:, :],
                                                start=True, stop=True)
                    last.then_inc(ss_mm, 1)

                def spread_norms(b, before):
                    pe.wait_ge(rn_done, 2 * b + 2)
                    for h in range(2):
                        if before:
                            free_T(before, h)
                        for n in range(4):
                            dst = psT[:, h, n * P:n * P + P]
                            col = 4 * h + n
                            nc.tensor.matmul(dst, rn[0][:, col:col + 1].broadcast_to([P, P]), ident_r[:, :],
                                             start=True, stop=False)
                            last = nc.tensor.matmul(dst, rn[1][:, col:col + 1].broadcast_to([P, P]), ident_r[:, :],
                                                    start=False, stop=True)
                        last.then_inc(rn_mm, 1)

                def body(b, head, tail, nxt):
                    if head:
                        mm_k(b, 0)
                    if tail:
                        tr_q(b - 1, 3, ("q", b - 1, 2))
                        context(b - 1)
                    if head:
                        tr_c(b, ("q", b - 1, 3) if tail else None)
                        mm_q(b, 0)
                    if tail:
                        fold(b - 1)
                    if head:
                        tr_k(b, 0, ("c", b, 0))
                        mm_k(b, 1)
                        shift_q(b, 0)
                    if tail:
                        output(b - 1, 0)
                    if head:
                        mm_q(b, 1)
                        tr_k(b, 1, ("k", b, 0))
                    if tail:
                        output(b - 1, 1)
                    if head:
                        shift_q(b, 1)
                        mm_k(b, 2)
                        tr_q(b, 0, ("k", b, 1))
                    if tail:
                        square_norms(b - 1)
                    if head:
                        mm_q(b, 2)
                        tr_k(b, 2, ("q", b, 0))
                        mm_k(b, 3)
                    if tail:
                        spread_norms(b - 1, ("k", b, 2) if head else ("q", b - 1, 3))
                    if head:
                        shift_q(b, 2)
                        tr_q(b, 1, ("r", b - 1, 0) if tail else ("k", b, 2))
                        mm_q(b, 3)
                        tr_k(b, 3, ("q", b, 1))
                        shift_q(b, 3)
                        tr_q(b, 2, ("k", b, 3))

                run(pe, body)

        ffn_phase(nc, outer, ident, ident_r, gates, ps, started, wait_apart, rsqrt_chain, three_pass, A, B, Wr, x2_dram, out)


def ffn_phase(nc, outer, ident, ident_r, gates, ps, started, wait_apart, rsqrt_chain, three_pass, A, B, Wr, x2_dram, out):
    f32 = mybir.dt.float32
    f32r = mybir.dt.float32r
    ALU = mybir.AluOpType
    ACT = mybir.ActivationFunctionType
    AX = mybir.AxisListType
    NB, T, D = out.shape
    E, R = A.shape[0], A.shape[1]
    KR = E * R
    P = 128
    DC = D // P
    KC = KR // P
    EC = E // KC
    SCALING = 32.0 / R
    LN_EPS = 1e-5
    NEWTON, NCH = 3, 11
    NEG = -3.0e38
    ND = P // 16
    with ExitStack() as ph:
        def sb(name, shape, dt=f32):
            return ph.enter_context(nc.sbuf_tensor(name, shape, dt))

        def sem(name):
            return ph.enter_context(nc.semaphore(name))

        NSTG = 4
        stage = sb("stage", [P, NSTG, D])
        b_stage = sb("b_stage", [P, 2, D])
        wr_stage = sb("wr_stage", [E, D])
        aT = [sb("aT_hi", [P, DC, KR], f32r), sb("aT_lo", [P, DC, KR], f32r)]
        bT = [sb("bT_hi", [P, KC, D], f32r), sb("bT_lo", [P, KC, D], f32r)]
        wrT = [sb("wrT_hi", [P, DC, E], f32r), sb("wrT_lo", [P, DC, E], f32r)]
        gf = sb("gf", [P, 1])
        x2b = sb("x2b", [P, 2, D])
        y = sb("y", [P, D])
        yT = [sb("yT_hi", [P, DC, T], f32r), sb("yT_lo", [P, DC, T], f32r)]
        hg = sb("hg", [P, KR])
        hT = [sb("hT_hi", [P, KC, T], f32r), sb("hT_lo", [P, KC, T], f32r)]
        res = sb("res", [P, 2, D])
        bn = sb("bn2", [P, 2, 6])
        mv = sb("mv2", [P, 2])
        s1, y1, t1 = sb("s1", [P, 1]), sb("y1", [P, 1]), sb("t1", [P, 1])
        nb1 = sb("nb1", [P, 1])
        sc = sb("sc", [P, E])
        top8 = sb("top8", [P, 2, 8])
        rest = sb("rest", [P, 2, E])
        neg_top = sb("neg_top", [P, 1])
        ex = sb("ex", [P, E])
        gsel = sb("gsel", [P, E])
        gsum = sb("gsum", [P, 1])
        grec = sb("grec", [P, 1])
        gate = sb("gate", [P, E])

        dve_turns = sem("dve2_turns")
        st_loaded = [sem(f"st_loaded{n}") for n in range(NSTG)]
        wr_loaded = sem("wr_loaded")
        w_T, w_hi, w_lo, gf_done = sem("w2_T"), sem("w2_hi"), sem("w2_lo"), sem("gf_done")
        b_ready = sem("b_ready")
        x2_loaded = [sem("x2_loaded0"), sem("x2_loaded1")]
        out_stored = [sem("out_stored0"), sem("out_stored1")]
        stats_step, newton_step, nb_done, y_done = (
            sem("stats2_step"), sem("newton2_step"), sem("nb2_done"), sem("y_done"))
        y_T, y_hi, y_lo = sem("y_T"), sem("y_hi"), sem("y_lo")
        sc_mm, top_step, sc_exp = sem("sc_mm"), sem("top_step"), sem("sc_exp")
        h_mm, hg_done, h_T, h_hi, h_lo = (
            sem("h_mm"), sem("hg_done"), sem("h_T"), sem("h_hi"), sem("h_lo"))
        f_mm, res_done = sem("f_mm"), sem("res_done")
        psH, psF, psT, psS = ps[:, 0:2, :], ps[:, 2:4, :], ps[:, 4:6, :], ps[:, 6, 0:E]
        TB = 8
        TOP = 11

        a_rows = A.rearrange("(k e) r d -> k (e r) d", e=EC)
        b_rows = B.rearrange("(k e) (p d) r -> k p e (d r)", e=EC, d=ND)
        tasks = [("a", k) for k in range(KC)] + [("b", k) for k in range(KC)]

        block = ph.enter_context(nc.Block())

        @block.sync
        def _(sp):
            sp.dma_start(wr_stage[:, :], Wr).then_inc(wr_loaded, 16)
            for t, (kind, k) in enumerate(tasks):
                if t >= NSTG and tasks[t - NSTG][0] == "a":
                    sp.wait_ge(w_T, 2 * (t - NSTG) + 2)
                elif t >= NSTG:
                    sp.wait_ge(b_ready, tasks[t - NSTG][1] + 1)
                if kind == "a":
                    sp.dma_start(stage[:, t % NSTG, :], a_rows[k]).then_inc(st_loaded[t % NSTG], 16)
                else:
                    sp.dma_start(stage[:, t % NSTG, :].rearrange("p (e w) -> p e w", e=EC),
                                 b_rows[k]).then_inc(st_loaded[t % NSTG], 16)

            def load(b, half, value):
                sp.dma_start(x2b[:, half, :],
                             x2_dram[bass.ds(b, 1)].rearrange("o p n -> (o p) n")).then_inc(x2_loaded[half], 16)

            load(0, 0, 0)
            load(1, 1, 0)

            def pair(i, last):
                for half in range(2):
                    b = 2 * i + half
                    sp.wait_ge(res_done, 2 * b + 2)
                    sp.dma_start(out[bass.ds(b, 1)].rearrange("o p n -> (o p) n"),
                                 res[:, half, :]).then_inc(out_stored[half], 16)
                    if not last:
                        load(b + 2, half, 0)

            with sp.Fori(0, NB // 2 - 1) as i:
                pair(i, False)
            pair(NB // 2 - 1, True)
            for half in range(2):
                sp.wait_ge(out_stored[half], 16 * (NB // 2))

        def weight_part(part, kind, k, h, u):
            bank = ps[:, u % TB, :]
            if kind == "a":
                return (aT[part][:, 4 * h:4 * h + 4, k * P:k * P + P], bank.rearrange("p (n r) -> p n r", r=P))
            dst = bT[part][:, k, :].rearrange("p (q d) -> p q d", d=ND)[:, :, 4 * h:4 * h + 4]
            return dst, bank.rearrange("p (n q) -> p q n", q=P)

        @block.tensor
        def _(pe):
            for t, (kind, k) in enumerate(tasks):
                if kind == "a":
                    pe.wait_ge(st_loaded[t % NSTG], 16 * (t // NSTG + 1))
                else:
                    pe.wait_ge(b_ready, k + 1)
                for h in range(2):
                    u = 2 * t + h
                    if u >= TB:
                        pe.wait_ge(w_lo, u - TB + 1)
                    for n in range(4):
                        m = 4 * h + n
                        if kind == "a":
                            src = stage[:, t % NSTG, m * P:m * P + P]
                        else:
                            src = b_stage[:, k % 2, m * P:m * P + P]
                        last = nc.tensor.transpose(ps[:, u % TB, n * P:n * P + P], src, ident[:, :])
                    last.then_inc(w_T, 1)
            pe.wait_ge(wr_loaded, 16)
            u = 2 * len(tasks)
            pe.wait_ge(w_lo, u - TB + 1)
            for m in range(DC):
                last = nc.tensor.transpose(ps[:, u % TB, m * E:m * E + E], wr_stage[:, m * P:m * P + P],
                                           ident[0:E, 0:E])
            last.then_inc(w_T, 1)
            pe.wait_ge(w_lo, u + 1)

            def tr_y(b, before):
                pe.wait_ge(y_done, b + 1)
                for h in range(2):
                    if before is not None:
                        pe.wait_ge(h_lo, 2 * before + h + 1)
                    for n in range(4):
                        w = (4 * h + n) * P
                        last = nc.tensor.transpose(psT[:, h, n * P:n * P + P], y[:, w:w + P], ident[:, :])
                    last.then_inc(y_T, 1)

            def scores(b):
                pe.wait_ge(y_lo, 2 * b + 2)
                if started(b):
                    pe.wait_ge(top_step, TOP * (b - 1) + 1)
                for m in range(DC):
                    last = three_pass(psS, yT[0][:, m, :], yT[1][:, m, :], wrT[0][:, m, :], wrT[1][:, m, :],
                                      m == 0, m == DC - 1)
                last.then_inc(sc_mm, 1)

            def up(b, g):
                if started(b):
                    pe.wait_ge(hg_done, 2 * b - 2 + g + 1)
                v = slice(512 * g, 512 * g + 512)
                for m in range(DC):
                    last = three_pass(psH[:, g, :], yT[0][:, m, :], yT[1][:, m, :], aT[0][:, m, v], aT[1][:, m, v],
                                      m == 0, m == DC - 1)
                last.then_inc(h_mm, 1)

            def tr_h(b, g, nxt):
                pe.wait_ge(hg_done, 2 * b + g + 1)
                if nxt:
                    pe.wait_ge(y_lo, 2 * b + 2 + g + 1)
                elif not nxt:
                    pe.wait_ge(h_lo, 2 * b - 2 + g + 1)
                for n in range(4):
                    w = (4 * g + n) * P
                    last = nc.tensor.transpose(psT[:, g, n * P:n * P + P], hg[:, w:w + P], ident[:, :])
                last.then_inc(h_T, 1)

            def down(b, g):
                if started(b):
                    pe.wait_ge(res_done, 2 * b - 2 + g + 1)
                v = slice(512 * g, 512 * g + 512)
                for m in range(KC):
                    if g == 0 and m in (0, KC // 2):
                        pe.wait_ge(h_lo, 2 * b + 1 + m // (KC // 2))
                    last = three_pass(psF[:, g, :], hT[0][:, m, :], hT[1][:, m, :], bT[0][:, m, v], bT[1][:, m, v],
                                      m == 0, m == KC - 1)
                last.then_inc(f_mm, 1)

            tr_y(0, None)
            scores(0)

            def body(b, nxt):
                up(b, 0)
                up(b, 1)
                if nxt:
                    tr_y(b + 1, None if isinstance(b, int) and b == 0 else b - 1)
                tr_h(b, 0, nxt)
                tr_h(b, 1, nxt)
                if nxt:
                    scores(b + 1)
                down(b, 0)
                down(b, 1)

            body(0, True)
            with pe.Fori(1, NB - 1) as b:
                body(b, True)
            body(NB - 1, False)

        @block.scalar
        def _(act):
            nc.scalar.activation(gf[:, :], gates[:, 1:2], ACT.Copy, scale=SCALING).then_inc(gf_done, 1)
            for t, (kind, k) in enumerate(tasks):
                for h in range(2):
                    u = 2 * t + h
                    act.wait_ge(w_T, u + 1)
                    dst, src = weight_part(0, kind, k, h, u)
                    nc.scalar.activation(dst, src, ACT.Copy).then_inc(w_hi, 1)
            u = 2 * len(tasks)
            act.wait_ge(w_T, u + 1)
            nc.scalar.activation(wrT[0][:, :, :].rearrange("p a b -> p (a b)"), ps[:, u % TB, :],
                                 ACT.Copy).then_inc(w_hi, 1)

            def normalise(b, half):
                act.wait_ge(nb_done, b + 1)
                if started(b):
                    act.wait_ge(y_T, 2 * b)
                nc.scalar.activation(y[:, :], x2b[:, half, :], ACT.Identity, bias=nb1[:, 0:1],
                                     scale=y1[:, 0:1]).then_inc(y_done, 1)

            def hi_y(b):
                for h in range(2):
                    act.wait_ge(y_T, 2 * b + h + 1)
                    nc.scalar.activation(yT[0][:, 4 * h:4 * h + 4, :],
                                         psT[:, h, :].rearrange("p (n c) -> p n c", c=P),
                                         ACT.Copy).then_inc(y_hi, 1)

            def exp_scores(b):
                act.wait_ge(top_step, TOP * b + 3)
                nc.scalar.activation(ex[:, :], sc[:, :], ACT.Exp, bias=neg_top[:, 0:1]).then_inc(sc_exp, 1)

            def body(b, half, nxt):
                if nxt:
                    normalise(b + 1, 1 - half)
                    hi_y(b + 1)
                for g in range(2):
                    act.wait_ge(h_T, 2 * b + g + 1)
                    nc.scalar.activation(hT[0][:, 4 * g:4 * g + 4, :],
                                         psT[:, g, :].rearrange("p (n c) -> p n c", c=P),
                                         ACT.Copy).then_inc(h_hi, 1)
                if nxt:
                    exp_scores(b + 1)

            normalise(0, 0)
            hi_y(0)
            exp_scores(0)
            body(0, 0, True)
            with act.Fori(0, NB // 2 - 1) as i:
                body(2 * i + 1, 1, True)
                body(2 * i + 2, 0, True)
            body(NB - 1, 1, False)

        @block.vector
        def _(dve):
            def reorder(k):
                t = KC + k
                dve.wait_ge(st_loaded[t % NSTG], 16 * (t // NSTG + 1))
                if k >= 2:
                    dve.wait_ge(w_T, 2 * (t - 2) + 2)
                nc.vector.tensor_copy(b_stage[:, k % 2, :].rearrange("p (d e r) -> p e d r", e=EC, d=ND),
                                      stage[:, t % NSTG, :].rearrange("p (e d r) -> p e d r", e=EC, d=ND)
                                      ).then_inc(b_ready, 1)

            for t, (kind, k) in enumerate(tasks):
                if t + 1 >= KC and t + 1 < 2 * KC:
                    reorder(t + 1 - KC)
                for h in range(2):
                    u = 2 * t + h
                    dve.wait_ge(w_hi, u + 1)
                    dst, src = weight_part(1, kind, k, h, u)
                    hi, _ = weight_part(0, kind, k, h, u)
                    nc.vector.tensor_tensor(dst, src, hi.bitcast(f32), ALU.subtract).then_inc(w_lo, 1)
            u = 2 * len(tasks)
            dve.wait_ge(w_hi, u + 1)
            nc.vector.tensor_tensor(wrT[1][:, :, :].rearrange("p a b -> p (a b)"), ps[:, u % TB, :],
                                    wrT[0][:, :, :].rearrange("p a b -> p (a b)").bitcast(f32),
                                    ALU.subtract).then_inc(w_lo, 1)
            dve.wait_ge(gf_done, 1)
            NS = 4

            def stats(b, half, value):
                dve.wait_ge(x2_loaded[half], value)
                for h in range(2):
                    nc.vector.bn_stats(bn[:, h, :], x2b[:, half, 512 * h:512 * h + 512]).then_inc(stats_step, 1)
                wait_apart(dve, dve_turns, (stats_step, NS * b + 2), *([(y_done, b)] if started(b) else []))
                nc.vector.bn_aggr(mv[:, :], bn[:, :, :].rearrange("p a b -> p (a b)")).then_inc(stats_step, 1)
                dve.wait_ge(stats_step, NS * b + 3)
                nc.vector.tensor_scalar(s1[:, :], mv[:, 1:2], LN_EPS, None, ALU.add).then_inc(stats_step, 1)
                dve.wait_ge(stats_step, NS * b + 4)
                rsqrt_chain(dve, y1[:, :], t1[:, :], s1[:, :], newton_step, NCH * b)
                dve.wait_ge(newton_step, NCH * (b + 1))
                nc.vector.scalar_tensor_tensor(nb1[:, :], mv[:, 0:1], -1.0, y1[:, :], ALU.mult,
                                               ALU.mult).then_inc(nb_done, 1)

            def lo_y(b):
                for h in range(2):
                    dve.wait_ge(y_hi, 2 * b + h + 1)
                    nc.vector.tensor_tensor(yT[1][:, 4 * h:4 * h + 4, :],
                                            psT[:, h, :].rearrange("p (n c) -> p n c", c=P),
                                            yT[0][:, 4 * h:4 * h + 4, :].bitcast(f32),
                                            ALU.subtract).then_inc(y_lo, 1)

            def route(b):
                step = [0]

                def link(ins, alone=False):
                    step[0] += 1
                    ins.then_inc(top_step, 1)
                    if alone:
                        wait_apart(dve, dve_turns, (top_step, TOP * b + step[0]))
                    else:
                        dve.wait_ge(top_step, TOP * b + step[0])

                dve.wait_ge(sc_mm, b + 1)
                link(nc.vector.tensor_copy(sc[:, :], psS), True)
                link(nc.vector.max(top8[:, 0, :], sc[:, :]))
                link(nc.vector.tensor_scalar(neg_top[:, :], top8[:, 0, 0:1], -1.0, None, ALU.mult), True)
                link(nc.vector.match_replace(rest[:, 0, :], top8[:, 0, :], sc[:, :], NEG), True)
                link(nc.vector.max(top8[:, 1, :], rest[:, 0, :]), True)
                link(nc.vector.match_replace(rest[:, 1, :], top8[:, 1, :], rest[:, 0, :], NEG))
                link(nc.vector.tensor_tensor(gsel[:, :], sc[:, :], rest[:, 1, :], ALU.not_equal))
                dve.wait_ge(sc_exp, b + 1)
                link(nc.vector.tensor_tensor(gsel[:, :], gsel[:, :], ex[:, :], ALU.mult))
                link(nc.vector.tensor_reduce(gsum[:, :], gsel[:, :], axis=AX.X, op=ALU.add))
                link(nc.vector.reciprocal(grec[:, :], gsum[:, :]))
                link(nc.vector.tensor_scalar(gate[:, :], gsel[:, :], grec[:, 0:1], None, ALU.mult))
                assert step[0] == TOP

            def gated(b, g):
                dve.wait_ge(h_mm, 2 * b + g + 1)
                if started(b):
                    dve.wait_ge(h_T, 2 * b)
                n = 512 // R
                nc.vector.tensor_tensor(hg[:, 512 * g:512 * g + 512].rearrange("p (e r) -> p e r", r=R),
                                        psH[:, g, :].rearrange("p (e r) -> p e r", r=R),
                                        gate[:, n * g:n * g + n].unsqueeze(2).broadcast_to([P, n, R]),
                                        ALU.mult).then_inc(hg_done, 1)

            def lo_h(b):
                for g in range(2):
                    dve.wait_ge(h_hi, 2 * b + g + 1)
                    nc.vector.tensor_tensor(hT[1][:, 4 * g:4 * g + 4, :],
                                            psT[:, g, :].rearrange("p (n c) -> p n c", c=P),
                                            hT[0][:, 4 * g:4 * g + 4, :].bitcast(f32),
                                            ALU.subtract).then_inc(h_lo, 1)

            def result(b, half, pairs):
                for g in range(2):
                    dve.wait_ge(f_mm, 2 * b + g + 1)
                    if g == 0 and started(pairs):
                        dve.wait_ge(out_stored[half], 16 * pairs)
                    v = slice(512 * g, 512 * g + 512)
                    nc.vector.scalar_tensor_tensor(res[:, half, v], psF[:, g, :], gf[:, 0:1], x2b[:, half, v],
                                                   ALU.mult, ALU.add).then_inc(res_done, 1)

            def body(b, half, pairs, nxt):
                if nxt:
                    loads = pairs + 1 + half
                    stats(b + 1, 1 - half, 16 * loads)
                gated(b, 0)
                gated(b, 1)
                if nxt:
                    lo_y(b + 1)
                lo_h(b)
                if nxt:
                    route(b + 1)
                result(b, half, pairs)

            stats(0, 0, 16)
            lo_y(0)
            route(0)
            body(0, 0, 0, True)
            body(1, 1, 0, True)
            with dve.Fori(1, NB // 2 - 1) as i:
                body(2 * i, 0, i, True)
                body(2 * i + 1, 1, i, True)
            body(NB - 2, 0, NB // 2 - 1, True)
            body(NB - 1, 1, NB // 2 - 1, False)


_INS = ["x", "ctx_4096", "g_xattn", "g_ffn", "L0_xattn_Wq", "L0_xattn_Wk", "L0_xattn_Wv", "L0_xattn_Wo",
        "L0_xattn_bo", "L0_xattn_g", "L0_ffn_A", "L0_ffn_B", "L0_ffn_Wr"]


def kernel(**inputs):
    import numpy as _np
    import concourse.bacc as _bacc
    from concourse import mybir as _mybir
    from concourse.bass_utils import run_bass_kernel_spmd as _run

    nc = _bacc.Bacc("TRN2", target_bir_lowering=False, num_devices=1)
    arrays, args = {}, []
    for name in _INS:
        a = _np.ascontiguousarray(inputs[name])
        arrays[f"in_{name}"] = a
        args.append(nc.dram_tensor(f"in_{name}", a.shape, _mybir.dt.from_np(a.dtype), kind="ExternalInput").ap())
    shape = tuple(inputs["x"].shape)
    scratch = nc.dram_tensor("x2_scratch", shape, _mybir.dt.float32, kind="Internal").ap()
    out = nc.dram_tensor("out_0", shape, _mybir.dt.float32, kind="ExternalOutput").ap()
    flamingo_layer(nc, *args, scratch, out)
    r = _run(nc, [arrays], core_ids=[0])
    return r.results[0]["out_0"]
```

```python
import concourse.bass as bass
from concourse import mybir
from contextlib import ExitStack
import math


def flamingo_layer(nc, x, ctx, g_xattn, g_ffn, Wq, Wk, Wv, Wo, bo, g, A, B, Wr, x2_dram, out):
    f32 = mybir.dt.float32
    f32r = mybir.dt.float32r
    i32 = mybir.dt.int32
    ALU = mybir.AluOpType
    ACT = mybir.ActivationFunctionType
    AX = mybir.AxisListType

    NB, C, N = x.shape
    HD = Wq.shape[0]
    DH = 64
    P = 128
    H = HD // DH
    CH = HD // P
    BK = N // P
    HF = N // 512
    E, R = A.shape[0], A.shape[1]
    KR = E * R
    LN_EPS = 1e-5
    MIN_SS = 1e-24
    MAGIC = 1597463007
    NEWTON = 3
    NCH = 2 + 3 * NEWTON
    NEG = -3.0e38

    def started(b):
        return not (isinstance(b, int) and b == 0)

    def wait_apart(eng, turns, *waits):
        for sem, value in waits:
            eng.wait_ge(sem, value)
        eng.sem_inc(turns, 1)

    def rsqrt_step(dve, k, y, t, s, sem, base):
        if k > 0:
            dve.wait_ge(sem, base + k)
        if k == 0:
            last = nc.vector.tensor_scalar(t.bitcast(i32), s.bitcast(i32), 1, None, ALU.logical_shift_right)
        elif k == 1:
            last = nc.vector.tensor_scalar(y.bitcast(i32), t.bitcast(i32), -1.0, float(MAGIC), ALU.mult, ALU.add)
        elif k % 3 == 2:
            last = nc.vector.tensor_tensor(t, y, s, ALU.mult)
        elif k % 3 == 0:
            last = nc.vector.scalar_tensor_tensor(t, t, -0.5, y, ALU.mult, ALU.mult)
        else:
            last = nc.vector.scalar_tensor_tensor(y, t, 1.5, y, ALU.add, ALU.mult)
        last.then_inc(sem, 1)

    def three_pass(psum, whi, wlo, mhi, mlo, start, stop):
        nc.tensor.matmul(psum, whi, mhi, start=start, stop=False)
        nc.tensor.matmul(psum, wlo, mhi, start=False, stop=False)
        return nc.tensor.matmul(psum, whi, mlo, start=False, stop=stop)

    outer = ExitStack()
    with outer:
        def const(name, shape, dt=f32):
            return outer.enter_context(nc.sbuf_tensor(name, shape, dt))

        def osem(name):
            return outer.enter_context(nc.semaphore(name))

        ident = const("ident", [P, P])
        ident_r = const("ident_r", [P, P], f32r)
        gates = const("gates", [P, 2])
        stage = const("stage", [P, 4, A.shape[2]])
        st_loaded = [osem(f"st_loaded{n}") for n in range(4)]
        ps = outer.enter_context(nc.psum_tensor("ps", [P, 8, 512], f32))
        psK = ps[:, 0:2, :]
        psQ = ps[:, 2:4, :]
        psT = ps[:, 4:6, :]
        psX = ps[:, 6:8, :]

        with ExitStack() as ph:
            def sb(name, shape, dt=f32):
                return ph.enter_context(nc.sbuf_tensor(name, shape, dt))

            def sem(name):
                return ph.enter_context(nc.semaphore(name))

            wstage = sb("wstage", [P, 4, CH, P])
            wk = [sb("wk_hi", [P, HD], f32r), sb("wk_lo", [P, HD], f32r)]
            wq = [sb("wq_hi", [P, HD], f32r), sb("wq_lo", [P, HD], f32r)]
            woT = sb("woT", [P, CH, P])
            wvo = [sb("wvo_hi", [P, CH, 2 * P], f32r), sb("wvo_lo", [P, CH, 2 * P], f32r)]
            g_raw = sb("g_raw", [P, 4])
            gcol = sb("gcol", [P, 1])
            ones = sb("ones", [P, 1])
            ctx_in = sb("ctx_in", [P, N])
            x_in = sb("x_in", [P, N])
            x_res = sb("x_res", [P, N])
            cx = [sb("ctx_hi", [P, N], f32r), sb("ctx_lo", [P, N], f32r)]
            xn = sb("xn", [P, N])
            xs = [sb("xn_hi", [P, N], f32r), sb("xn_lo", [P, N], f32r)]
            cT = [sb("ctxT_hi", [P, BK, C], f32r), sb("ctxT_lo", [P, BK, C], f32r)]
            ek = sb("ek", [P, 2, N])
            ekT = [sb("ekT_hi", [P, BK, HD], f32r), sb("ekT_lo", [P, BK, HD], f32r)]
            kmax = sb("kmax", [P, CH])
            ksum = sb("ksum", [P, CH])
            krec = sb("krec", [P, CH])
            qe = sb("qe", [P, 2, 2 * HD])
            qmax = sb("qmax", [P, 2, 2 * H], f32r)
            qsum = sb("qsum", [P, 2, 2 * H])
            qrec = sb("qrec", [P, 2, 2 * H])
            qT = [sb("qT_hi", [P, CH, N], f32r), sb("qT_lo", [P, CH, N], f32r)]
            kc = [sb("kc_hi", [P, HD], f32r), sb("kc_lo", [P, HD], f32r)]
            mt = sb("mt", [P, CH, P])
            mts = [sb("mt_hi", [P, CH, P], f32r), sb("mt_lo", [P, CH, P], f32r)]
            osb = sb("osb", [P, N])
            osq = sb("osq", [P, N])
            usb = sb("usb", [P, N])
            x2 = sb("x2", [P, N])
            bn = sb("bn", [P, HF, 6])
            mv = sb("mv", [P, 2])
            var, var_y, var_t = sb("var", [P, 1]), sb("var_y", [P, 1]), sb("var_t", [P, 1])
            ss, ss_y, ss_t = sb("ss", [P, BK]), sb("ss_y", [P, BK]), sb("ss_t", [P, BK])
            nbias = sb("nbias", [P, 1])
            rn = [sb("rn_hi", [P, BK], f32r), sb("rn_lo", [P, BK], f32r)]

            dve_turns, sp_turns = sem("dve_turns"), sem("sp_turns")
            w_loaded, id_ready, ones_ready = sem("w_loaded"), sem("id_ready"), sem("ones_ready")
            wT_done, w_hi, w_lo = sem("wT_done"), sem("w_hi"), sem("w_lo")
            fold_done, fold_hi, fold_lo = sem("fold_done"), sem("fold_hi"), sem("fold_lo")
            tanh_done, gcol_done = sem("tanh_done"), sem("gcol_done")
            ctx_loaded, x_loaded, xres_loaded, x2_stored = (
                sem("ctx_loaded"), sem("x_loaded"), sem("xres_loaded"), sem("x2_stored"))
            ctx_hi, ctx_lo, xn_hi, xn_lo = sem("ctx_hi"), sem("ctx_lo"), sem("xn_hi"), sem("xn_lo")
            stats_step, var_step, nbias_done, xn_done = (
                sem("stats_step"), sem("var_step"), sem("nbias_done"), sem("xn_done"))
            k_mm, k_max, k_exp, k_T, k_hi, k_lo, k_rec = (
                sem("k_mm"), sem("k_max"), sem("k_exp"), sem("k_T"), sem("k_hi"), sem("k_lo"),
                sem("k_rec"))
            q_mm, q_max, q_shift, q_exp, q_sum, q_rec, q_norm, q_T, q_hi, q_lo = (
                sem("q_mm"), sem("q_max"), sem("q_shift"), sem("q_exp"), sem("q_sum"),
                sem("q_rec"), sem("q_norm"), sem("q_T"), sem("q_hi"), sem("q_lo"))
            c_T, c_hi, c_lo = sem("c_T"), sem("c_hi"), sem("c_lo")
            kc_mm, kc_hi, kc_lo = sem("kc_mm"), sem("kc_hi"), sem("kc_lo")
            m_mm, m_scaled, m_hi, m_lo = sem("m_mm"), sem("m_scaled"), sem("m_hi"), sem("m_lo")
            o_mm, o_out, ss_mm, ss_read, ss_step, rn_done, rn_mm, u_done, x2_done = (
                sem("o_mm"), sem("o_out"), sem("ss_mm"), sem("ss_read"), sem("ss_step"), sem("rn_done"),
                sem("rn_mm"), sem("u_done"), sem("x2_done"))

            def run(eng, body):
                body(0, head=True, tail=False, late=False, ahead=True)
                body(1, head=True, tail=True, late=False, ahead=True)
                with eng.Fori(2, NB - 1) as b:
                    body(b, head=True, tail=True, late=True, ahead=True)
                body(NB - 1, head=True, tail=True, late=True, ahead=False)
                body(NB, head=False, tail=True, late=True, ahead=False)
                body(NB + 1, head=False, tail=False, late=True, ahead=False)

            block = ph.enter_context(nc.Block())

            @block.sync
            def _(sp):
                def load(dst, src, b, s):
                    sp.dma_start(dst, src[bass.ds(b, 1)].rearrange("o p n -> (o p) n")).then_inc(s, 16)

                load(ctx_in[:, :], ctx, 0, ctx_loaded)
                load(x_in[:, :], x, 0, x_loaded)
                load(x_res[:, :], x, 0, xres_loaded)
                sp.wait_ge(xn_done, 1)
                load(x_in[:, :], x, 1, x_loaded)
                for t in range(4):
                    load_weight_rows(sp, t, A, B, stage, st_loaded, None, None)

                def body(b, head, tail, late, ahead):
                    if late:
                        wait_apart(sp, sp_turns, (x2_done, b - 1))
                        sp.dma_start(x2_dram[bass.ds(b - 2, 1)].rearrange("o p n -> (o p) n"),
                                     x2[:, :]).then_inc(x2_stored, 16)
                        if tail:
                            load(x_res[:, :], x, b - 1, xres_loaded)
                    if ahead:
                        wait_apart(sp, sp_turns, (c_T, 2 * b + 2))
                        wait_apart(sp, sp_turns, (ctx_lo, b + 1))
                        load(ctx_in[:, :], ctx, b + 1, ctx_loaded)
                        if not (isinstance(b, int) and b == NB - 2):
                            wait_apart(sp, sp_turns, (xn_done, b + 2))
                            load(x_in[:, :], x, b + 2, x_loaded)

                body(0, head=True, tail=False, late=False, ahead=True)
                body(1, head=True, tail=True, late=False, ahead=True)
                with sp.Fori(2, NB - 2) as b:
                    body(b, head=True, tail=True, late=True, ahead=True)
                body(NB - 2, head=True, tail=True, late=True, ahead=True)
                body(NB - 1, head=True, tail=True, late=True, ahead=False)
                body(NB, head=False, tail=True, late=True, ahead=False)
                body(NB + 1, head=False, tail=False, late=True, ahead=False)
                sp.wait_ge(x2_stored, 16 * NB)

            @block.gpsimd
            def _(pool):
                nc.gpsimd.memset(ident[:, :], 0.0).then_inc(id_ready, 1)
                pool.wait_ge(id_ready, 1)
                nc.gpsimd.affine_select(out=ident[:, :], in_=ident[:, :], compare_op=ALU.not_equal,
                                        fill=1.0, base=0, pattern=[[-1, P]],
                                        channel_multiplier=1).then_inc(id_ready, 1)
                pool.wait_ge(id_ready, 2)
                nc.gpsimd.tensor_scalar(ident_r[:, :], ident[:, :], 1.0, 0.0, ALU.mult,
                                        ALU.add).then_inc(id_ready, 1)
                nc.gpsimd.memset(ones[:, :], 1.0).then_inc(ones_ready, 1)

                def lo_ctx(b):
                    pool.wait_ge(ctx_hi, b + 1)
                    nc.gpsimd.tensor_tensor(cx[1][:, :], ctx_in[:, :], cx[0][:, :].bitcast(f32),
                                            ALU.subtract).then_inc(ctx_lo, 1)

                def lo_xn(b, h):
                    pool.wait_ge(xn_hi, 2 * b + h + 1)
                    v = slice(512 * h, 512 * h + 512)
                    nc.gpsimd.tensor_tensor(xs[1][:, v], xn[:, v], xs[0][:, v].bitcast(f32),
                                            ALU.subtract).then_inc(xn_lo, 1)

                def normalise(b, p):
                    pool.wait_ge(q_rec, 4 * b + p + 1)
                    v = qe[:, p % 2, :].rearrange("p (h d) -> p h d", d=DH)
                    w = qrec[:, p % 2, :].unsqueeze(2).broadcast_to([P, 2 * H, DH])
                    nc.gpsimd.tensor_tensor(v, v, w, ALU.mult).then_inc(q_norm, 1)

                def finish(b):
                    pool.wait_ge(xres_loaded, 16 * (b + 1))
                    if started(b):
                        pool.wait_ge(x2_stored, 16 * b)
                    pool.wait_ge(u_done, 2 * b + 2)
                    nc.gpsimd.tensor_tensor(x2[:, :], usb[:, :], x_res[:, :], ALU.add).then_inc(x2_done, 1)

                def body(b, head, tail, late, ahead):
                    if tail:
                        normalise(b - 1, 3)
                    if late:
                        finish(b - 2)
                    if head:
                        normalise(b, 0)
                    if tail:
                        pool.wait_ge(m_hi, b)
                        nc.gpsimd.tensor_tensor(mts[1][:, :, :], mt[:, :, :], mts[0][:, :, :].bitcast(f32),
                                                ALU.subtract).then_inc(m_lo, 1)
                    if head:
                        normalise(b, 1)
                    if ahead:
                        lo_ctx(b + 1)
                        lo_xn(b + 1, 0)
                    if head:
                        normalise(b, 2)
                    if ahead:
                        lo_xn(b + 1, 1)

                lo_ctx(0)
                lo_xn(0, 0)
                lo_xn(0, 1)
                run(pool, body)

            @block.scalar
            def _(act):
                act.dma_start(wstage[:, 0, :, :], Wk.rearrange("(j p) c -> p j c", p=P)).then_inc(w_loaded, 16)
                act.dma_start(wstage[:, 1, :, :], Wq.rearrange("(j p) c -> p j c", p=P)).then_inc(w_loaded, 16)
                act.dma_start(wstage[:, 2, :, :], Wv.rearrange("(j p) c -> p j c", p=P)).then_inc(w_loaded, 16)
                act.dma_start(wstage[:, 3, :, :], Wo.rearrange("o (j c) -> o j c", c=P)).then_inc(w_loaded, 16)
                act.dma_start(g_raw[:, 0:1], g_xattn.rearrange("(a n) -> a n", a=1).broadcast_to([P, 1])).then_inc(w_loaded, 16)
                act.dma_start(g_raw[:, 1:2], g_ffn.rearrange("(a n) -> a n", a=1).broadcast_to([P, 1])).then_inc(w_loaded, 16)
                act.dma_start(g_raw[:, 2:3], g[0]).then_inc(w_loaded, 16)
                act.dma_start(g_raw[:, 3:4], bo.rearrange("(p a) -> p a", a=1)).then_inc(w_loaded, 16)
                act.wait_ge(w_loaded, 128)
                nc.scalar.activation(gates[:, :], g_raw[:, 0:2], ACT.Tanh).then_inc(tanh_done, 1)
                bo_col = g_raw[:, 3:4]

                act.wait_ge(wT_done, 1)
                nc.scalar.activation(wk[0][:, :], psT[:, 0, :], ACT.Copy).then_inc(w_hi, 1)
                act.wait_ge(wT_done, 2)
                nc.scalar.activation(wq[0][:, :], psT[:, 1, :], ACT.Copy).then_inc(w_hi, 1)
                act.wait_ge(wT_done, 3)
                nc.scalar.activation(woT[:, :, :].rearrange("p a b -> p (a b)"), psK[:, 0, :],
                                     ACT.Copy).then_inc(w_hi, 1)
                act.wait_ge(fold_done, 1)
                for par in range(2):
                    nc.scalar.activation(wvo[0][:, :, par * P:par * P + P],
                                         psX[:, par, :].rearrange("p (j o) -> p j o", o=P),
                                         ACT.Copy, scale=DH ** -0.5).then_inc(fold_hi, 1)

                def norm_x(b):
                    act.wait_ge(nbias_done, b + 1)
                    nc.scalar.activation(xn[:, :], x_in[:, :], ACT.Identity, bias=nbias[:, 0:1],
                                         scale=var_y[:, 0:1]).then_inc(xn_done, 1)

                def hi_ctx(b):
                    act.wait_ge(ctx_loaded, 16 * (b + 1))
                    if started(b):
                        act.wait_ge(k_mm, 4 * b)
                    nc.scalar.activation(cx[0][:, :], ctx_in[:, :], ACT.Copy).then_inc(ctx_hi, 1)

                def hi_xn(b, h):
                    if started(b):
                        act.wait_ge(q_mm, 4 * b - 4 + 2 * h + 2)
                    act.wait_ge(xn_done, b + 1)
                    v = slice(512 * h, 512 * h + 512)
                    nc.scalar.activation(xs[0][:, v], xn[:, v], ACT.Copy).then_inc(xn_hi, 1)

                hi_ctx(0)
                norm_x(0)
                hi_xn(0, 0)
                hi_xn(0, 1)

                def exp_k(b, j):
                    act.wait_ge(k_max, 4 * b + j + 1)
                    if j == 0 and started(b):
                        act.wait_ge(k_rec, b)
                    if j >= 2 or started(b):
                        act.wait_ge(k_T, 8 * b + 2 * j - 2)
                    nc.scalar.activation(ek[:, j % 2, :].rearrange("p (a n) -> p a n", a=HF), psK,
                                         ACT.Exp, bias=kmax[:, j:j + 1],
                                         accum_out=ksum[:, j:j + 1]).then_inc(k_exp, 1)

                def exp_q(b, p):
                    act.wait_ge(q_shift, 4 * b + p + 1)
                    if p >= 2 or started(b):
                        act.wait_ge(q_T, 8 * b + 2 * p - 2)
                    nc.scalar.activation(qe[:, p % 2, :].rearrange("p (a n) -> p a n", a=2), psQ,
                                         ACT.Exp).then_inc(q_exp, 1)

                def hi_q(b, p):
                    for h in range(2):
                        act.wait_ge(q_T, 8 * b + 2 * p + h + 1)
                        nb = 2 * p + h
                        nc.scalar.activation(qT[0][:, :, nb * P:nb * P + P],
                                             psT[:, h, :].rearrange("p (j n) -> p j n", n=P),
                                             ACT.Copy).then_inc(q_hi, 1)

                def hi_k(b, j):
                    for h in range(2):
                        act.wait_ge(k_T, 8 * b + 2 * j + h + 1)
                        nc.scalar.activation(ekT[0][:, 4 * h:4 * h + 4, j * P:j * P + P],
                                             psT[:, h, :].rearrange("p (n d) -> p n d", d=P),
                                             ACT.Copy).then_inc(k_hi, 1)

                def out_o(b, h):
                    act.wait_ge(o_mm, 2 * b + h + 1)
                    v = slice(512 * h, 512 * h + 512)
                    nc.scalar.activation(osb[:, v], psX[:, h, :], ACT.Identity, bias=bo_col)
                    nc.scalar.activation(osq[:, v], psX[:, h, :], ACT.Square, bias=bo_col).then_inc(o_out, 1)

                def body(b, head, tail, late, ahead):
                    if tail:
                        exp_q(b - 1, 3)
                    if head:
                        exp_k(b, 0)
                    if tail:
                        hi_q(b - 1, 2)
                        act.wait_ge(kc_mm, b)
                        nc.scalar.activation(kc[0][:, :], psX[:, 0, :], ACT.Copy).then_inc(kc_hi, 1)
                    if head:
                        exp_q(b, 0)
                        hi_k(b, 0)
                        for h in range(2):
                            act.wait_ge(c_T, 2 * b + h + 1)
                            nc.scalar.activation(cT[0][:, 4 * h:4 * h + 4, :],
                                                 psT[:, h, :].rearrange("p (n c) -> p n c", c=P),
                                                 ACT.Copy).then_inc(c_hi, 1)
                        exp_k(b, 1)
                    if tail:
                        act.wait_ge(m_scaled, 2 * b)
                        nc.scalar.activation(mts[0][:, :, :], mt[:, :, :], ACT.Copy).then_inc(m_hi, 1)
                        hi_q(b - 1, 3)
                    if head:
                        exp_q(b, 1)
                        exp_k(b, 2)
                    if tail:
                        out_o(b - 1, 0)
                    if head:
                        hi_k(b, 1)
                    if ahead:
                        act.wait_ge(xn_lo, 2 * b + 2)
                        norm_x(b + 1)
                        hi_xn(b + 1, 0)
                    if head:
                        hi_q(b, 0)
                        exp_k(b, 3)
                    if tail:
                        out_o(b - 1, 1)
                    if ahead:
                        hi_ctx(b + 1)
                    if head:
                        hi_k(b, 2)
                        exp_q(b, 2)
                        hi_q(b, 1)
                        hi_k(b, 3)
                    if ahead:
                        hi_xn(b + 1, 1)

                run(act, body)

            @block.vector
            def _(dve):
                dve.wait_ge(tanh_done, 1)
                nc.vector.scalar_tensor_tensor(gcol[:, :], g_raw[:, 2:3], math.sqrt(C), gates[:, 0:1],
                                               ALU.mult, ALU.mult).then_inc(gcol_done, 1)
                NS = HF + 2

                def stats(b):
                    dve.wait_ge(x_loaded, 16 * (b + 1))
                    for h in range(HF):
                        nc.vector.bn_stats(bn[:, h, :], x_in[:, 512 * h:512 * h + 512]).then_inc(stats_step, 1)
                    wait_apart(dve, dve_turns, (stats_step, NS * b + HF), *([(nbias_done, b)] if started(b) else []))
                    nc.vector.bn_aggr(mv[:, :], bn[:, :, :].rearrange("p a b -> p (a b)")).then_inc(stats_step, 1)
                    dve.wait_ge(stats_step, NS * b + HF + 1)
                    nc.vector.tensor_scalar(var[:, :], mv[:, 1:2], LN_EPS, None, ALU.add).then_inc(stats_step, 1)

                def rstd(b, *steps):
                    for k in steps:
                        if k == 0:
                            dve.wait_ge(stats_step, NS * (b + 1))
                        if k == 1 and started(b):
                            dve.wait_ge(xn_done, b)
                        rsqrt_step(dve, k, var_y[:, :], var_t[:, :], var[:, :], var_step, NCH * b)
                        if k == NCH - 1:
                            dve.wait_ge(var_step, NCH * (b + 1))
                            nc.vector.scalar_tensor_tensor(nbias[:, :], mv[:, 0:1], -1.0, var_y[:, :],
                                                           ALU.mult, ALU.mult).then_inc(nbias_done, 1)

                def rnorm(b, *steps):
                    for k in steps:
                        if k == -1:
                            dve.wait_ge(ss_mm, b + 1)
                            nc.vector.tensor_scalar(ss[:, :], psX[:, 0, 0:BK], MIN_SS, None,
                                                    ALU.max).then_inc(ss_read, 1)
                        elif k < NCH:
                            if k == 0:
                                dve.wait_ge(ss_read, b + 1)
                            rsqrt_step(dve, k, ss_y[:, :], ss_t[:, :], ss[:, :], ss_step, NCH * b)
                        elif k == NCH:
                            dve.wait_ge(ss_step, NCH * (b + 1))
                            nc.vector.tensor_copy(rn[0][:, :], ss_y[:, :]).then_inc(rn_done, 1)
                        else:
                            dve.wait_ge(rn_done, 2 * b + 1)
                            nc.vector.tensor_tensor(rn[1][:, :], ss_y[:, :], rn[0][:, :].bitcast(f32),
                                                    ALU.subtract).then_inc(rn_done, 1)

                stats(0)
                rstd(0, *range(NCH))
                for n, w in enumerate((wk, wq)):
                    dve.wait_ge(w_hi, n + 1)
                    nc.vector.tensor_tensor(w[1][:, :], psT[:, n, :], w[0][:, :].bitcast(f32),
                                            ALU.subtract).then_inc(w_lo, 1)
                for par in range(2):
                    dve.wait_ge(fold_hi, 2)
                    nc.vector.scalar_tensor_tensor(wvo[1][:, :, par * P:par * P + P],
                                                   psX[:, par, :].rearrange("p (j o) -> p j o", o=P), DH ** -0.5,
                                                   wvo[0][:, :, par * P:par * P + P].bitcast(f32),
                                                   ALU.mult, ALU.subtract).then_inc(fold_lo, 1)

                def max_k(b, j):
                    dve.wait_ge(k_mm, 4 * b + j + 1)
                    nc.vector.tensor_reduce(kmax[:, j:j + 1], psK, axis=AX.XY, op=ALU.max,
                                            negate=True).then_inc(k_max, 1)

                def max_q(b, p):
                    dve.wait_ge(q_mm, 4 * b + p + 1)
                    nc.vector.tensor_reduce(qmax[:, p % 2, :], psQ.rearrange("p a (h d) -> p (a h) d", d=DH),
                                            axis=AX.X, op=ALU.max, negate=True).then_inc(q_max, 1)

                def sum_q(b, p):
                    dve.wait_ge(q_exp, 4 * b + p + 1)
                    nc.vector.tensor_reduce(qsum[:, p % 2, :], qe[:, p % 2, :].rearrange("p (h d) -> p h d", d=DH),
                                            axis=AX.X, op=ALU.add).then_inc(q_sum, 1)
                    dve.wait_ge(q_sum, 4 * b + p + 1)
                    nc.vector.reciprocal(qrec[:, p % 2, :], qsum[:, p % 2, :]).then_inc(q_rec, 1)

                def lo_q(b, p, h):
                    dve.wait_ge(q_hi, 8 * b + 2 * p + h + 1)
                    v = slice((2 * p + h) * P, (2 * p + h + 1) * P)
                    nc.vector.tensor_tensor(qT[1][:, :, v], psT[:, h, :].rearrange("p (j n) -> p j n", n=P),
                                            qT[0][:, :, v].bitcast(f32), ALU.subtract).then_inc(q_lo, 1)

                def lo_k(b, j, h):
                    dve.wait_ge(k_hi, 8 * b + 2 * j + h + 1)
                    n, w = slice(4 * h, 4 * h + 4), slice(j * P, j * P + P)
                    nc.vector.tensor_tensor(ekT[1][:, n, w], psT[:, h, :].rearrange("p (n d) -> p n d", d=P),
                                            ekT[0][:, n, w].bitcast(f32), ALU.subtract).then_inc(k_lo, 1)

                def lo_c(b, h):
                    dve.wait_ge(c_hi, 2 * b + h + 1)
                    n = slice(4 * h, 4 * h + 4)
                    nc.vector.tensor_tensor(cT[1][:, n, :], psT[:, h, :].rearrange("p (n c) -> p n c", c=P),
                                            cT[0][:, n, :].bitcast(f32), ALU.subtract).then_inc(c_lo, 1)

                def scale_m(b, par):
                    dve.wait_ge(m_mm, b + 1)
                    dve.wait_ge(k_rec, b + 1)
                    v = psX.rearrange("p a (c w) -> p (a c) w", w=2 * P)
                    r = slice(DH * par, DH * par + DH)
                    nc.vector.tensor_tensor(mt[r, :, :], v[r, :, par * P:par * P + P],
                                            krec[r, :].unsqueeze(2).broadcast_to([DH, CH, P]),
                                            ALU.mult).then_inc(m_scaled, 1)

                def gated(b, h):
                    dve.wait_ge(rn_mm, 2 * b + h + 1)
                    v = slice(512 * h, 512 * h + 512)
                    nc.vector.scalar_tensor_tensor(usb[:, v], osb[:, v], gcol[:, 0:1], psT[:, h, :],
                                                   ALU.mult, ALU.mult).then_inc(u_done, 1)

                def body(b, head, tail, late, ahead):
                    if head:
                        max_k(b, 0)
                    if tail:
                        sum_q(b - 1, 3)
                    if head:
                        max_q(b, 0)
                    if late:
                        gated(b - 2, 0)
                        gated(b - 2, 1)
                    if ahead:
                        stats(b + 1)
                    if tail:
                        lo_q(b - 1, 2, 0)
                        lo_q(b - 1, 2, 1)
                        dve.wait_ge(kc_hi, b)
                        nc.vector.tensor_tensor(kc[1][:, :], psX[:, 0, :], kc[0][:, :].bitcast(f32),
                                                ALU.subtract).then_inc(kc_lo, 1)
                    if ahead:
                        rstd(b + 1, 0)
                    if head:
                        lo_k(b, 0, 0)
                    if ahead:
                        rstd(b + 1, 1)
                    if head:
                        lo_k(b, 0, 1)
                    if ahead:
                        rstd(b + 1, 2)
                    if head:
                        sum_q(b, 0)
                        max_k(b, 1)
                    if ahead:
                        rstd(b + 1, 3)
                    if tail:
                        scale_m(b - 1, 0)
                        scale_m(b - 1, 1)
                    if ahead:
                        rstd(b + 1, 4)
                    if head:
                        lo_c(b, 0)
                    if ahead:
                        rstd(b + 1, 5)
                    if head:
                        lo_c(b, 1)
                    if ahead:
                        rstd(b + 1, 6)
                    if head:
                        max_q(b, 1)
                    if ahead:
                        rstd(b + 1, 7)
                    if head:
                        max_k(b, 2)
                    if ahead:
                        rstd(b + 1, 8)
                    if tail:
                        lo_q(b - 1, 3, 0)
                    if ahead:
                        rstd(b + 1, 9)
                    if tail:
                        lo_q(b - 1, 3, 1)
                    if ahead:
                        rstd(b + 1, 10)
                    if head:
                        sum_q(b, 1)
                        lo_k(b, 1, 0)
                        lo_k(b, 1, 1)
                        max_k(b, 3)
                        lo_q(b, 0, 0)
                        lo_q(b, 0, 1)
                        max_q(b, 2)
                        lo_k(b, 2, 0)
                        lo_k(b, 2, 1)
                    if tail:
                        rnorm(b - 1, -1, 0)
                    if head:
                        sum_q(b, 2)
                    if tail:
                        rnorm(b - 1, 1)
                    if head:
                        lo_q(b, 1, 0)
                    if tail:
                        rnorm(b - 1, 2)
                    if head:
                        lo_q(b, 1, 1)
                    if tail:
                        rnorm(b - 1, 3, 4)
                    if head:
                        max_q(b, 3)
                    if tail:
                        rnorm(b - 1, 5, 6)
                    if head:
                        lo_k(b, 3, 0)
                    if tail:
                        rnorm(b - 1, 7, 8)
                    if head:
                        lo_k(b, 3, 1)
                    if tail:
                        rnorm(b - 1, 9, 10, 11, 12)
                    if head:
                        dve.wait_ge(k_exp, 4 * b + 4)
                        nc.vector.reciprocal(krec[:, :], ksum[:, :]).then_inc(k_rec, 1)

                run(dve, body)

            @block.tensor
            def _(pe):
                pe.wait_ge(id_ready, 3)
                pe.wait_ge(w_loaded, 128)
                for n, dst in ((0, psT[:, 0, :]), (1, psT[:, 1, :]), (3, psK[:, 0, :])):
                    for j in range(CH):
                        last = nc.tensor.transpose(dst[:, j * P:j * P + P], wstage[:, n, j, :], ident[:, :])
                    last.then_inc(wT_done, 1)
                pe.wait_ge(w_hi, 3)
                for par in range(2):
                    r = slice(DH * par, DH * par + DH)
                    for j in range(CH):
                        last = nc.tensor.matmul(psX[:, par, j * P:j * P + P], wstage[r, 2, j, :],
                                                woT[r, j, :], start=True, stop=True)
                last.then_inc(fold_done, 1)
                pe.wait_ge(w_lo, 2)
                pe.wait_ge(fold_lo, 2)
                pe.wait_ge(ones_ready, 1)

                def free_T(task, h):
                    if task is None:
                        return
                    kind, b, n = task
                    if kind == "c":
                        pe.wait_ge(c_lo, 2 * b + h + 1)
                    if kind == "k":
                        pe.wait_ge(k_lo, 8 * b + 2 * n + h + 1)
                    if kind == "q":
                        pe.wait_ge(q_lo, 8 * b + 2 * n + h + 1)
                    if kind == "r":
                        pe.wait_ge(u_done, 2 * b + h + 1)

                def mm_k(b, j):
                    if j == 0:
                        pe.wait_ge(ctx_lo, b + 1)
                    if j > 0:
                        pe.wait_ge(k_exp, 4 * b + j)
                    elif started(b):
                        pe.wait_ge(k_exp, 4 * b)
                    for h in range(HF):
                        v = slice(512 * h, 512 * h + 512)
                        w = slice(P * j, P * j + P)
                        last = three_pass(psK[:, h, :], wk[0][:, w], wk[1][:, w], cx[0][:, v], cx[1][:, v],
                                          True, True)
                    last.then_inc(k_mm, 1)

                def mm_q(b, p):
                    if p % 2 == 0:
                        pe.wait_ge(xn_lo, 2 * b + p // 2 + 1)
                    if p > 0:
                        pe.wait_ge(q_exp, 4 * b + p)
                    elif started(b):
                        pe.wait_ge(q_exp, 4 * b)
                    for h in range(2):
                        w = slice(P * (2 * p + h), P * (2 * p + h) + P)
                        last = three_pass(psQ[:, h, :], xs[0][:, w], xs[1][:, w], wq[0][:, :], wq[1][:, :],
                                          True, True)
                    last.then_inc(q_mm, 1)

                def shift_q(b, p):
                    pe.wait_ge(q_max, 4 * b + p + 1)
                    for h in range(2):
                        m = qmax[:, p % 2, h * H:h * H + H].unsqueeze(2).broadcast_to([P, H, DH])
                        last = nc.tensor.matmul(psQ[:, h, :], ident_r[:, :], m, start=False, stop=True,
                                                skip_group_check=True)
                    last.then_inc(q_shift, 1)

                def tr_c(b, before):
                    for h in range(2):
                        free_T(before, h)
                        for n in range(4):
                            w = (4 * h + n) * P
                            last = nc.tensor.transpose(psT[:, h, n * P:n * P + P], ctx_in[:, w:w + P], ident[:, :])
                        last.then_inc(c_T, 1)

                def tr_k(b, j, before):
                    pe.wait_ge(k_exp, 4 * b + j + 1)
                    for h in range(2):
                        free_T(before, h)
                        for n in range(4):
                            w = (4 * h + n) * P
                            last = nc.tensor.transpose(psT[:, h, n * P:n * P + P], ek[:, j % 2, w:w + P], ident[:, :])
                        last.then_inc(k_T, 1)

                def tr_q(b, p, before):
                    pe.wait_ge(q_norm, 4 * b + p + 1)
                    for h in range(2):
                        free_T(before, h)
                        for j in range(CH):
                            w = h * HD + j * P
                            last = nc.tensor.transpose(psT[:, h, j * P:j * P + P], qe[:, p % 2, w:w + P], ident[:, :])
                        last.then_inc(q_T, 1)

                def context(b, half):
                    if half == 0:
                        pe.wait_ge(k_lo, 8 * b + 8)
                        pe.wait_ge(c_lo, 2 * b + 2)
                        if started(b):
                            pe.wait_ge(ss_read, b)
                    for n in range(BK // 2 * half, BK // 2 * (half + 1)):
                        last = three_pass(psX[:, 0, :], cT[0][:, n, :], cT[1][:, n, :], ekT[0][:, n, :],
                                          ekT[1][:, n, :], n == 0, n == BK - 1)
                    if half == 1:
                        last.then_inc(kc_mm, 1)

                def fold(b):
                    pe.wait_ge(kc_lo, b + 1)
                    for j in range(CH):
                        w = slice(P * j, P * j + P)
                        last = three_pass(psX[:, j // 2, (j % 2) * 2 * P:(j % 2) * 2 * P + 2 * P],
                                          kc[0][:, w], kc[1][:, w], wvo[0][:, j, :], wvo[1][:, j, :], True, True)
                    last.then_inc(m_mm, 1)

                def output(b, h, chunks):
                    if h == 0:
                        pe.wait_ge(m_lo, b + 1)
                    if chunks[0] == 0:
                        pe.wait_ge(q_lo, 8 * b + 4 * h + 4)
                    v = slice(512 * h, 512 * h + 512)
                    for j in chunks:
                        last = three_pass(psX[:, h, :], mts[0][:, j, :], mts[1][:, j, :], qT[0][:, j, v],
                                          qT[1][:, j, v], j == 0, j == CH - 1)
                    if chunks[-1] == CH - 1:
                        last.then_inc(o_mm, 1)

                def square_norms(b):
                    pe.wait_ge(o_out, 2 * b + 2)
                    for n in range(BK):
                        last = nc.tensor.matmul(psX[:, 0, n:n + 1], osq[:, n * P:n * P + P], ones[:, :],
                                                start=True, stop=True)
                    last.then_inc(ss_mm, 1)

                def spread_norms(b, before):
                    pe.wait_ge(rn_done, 2 * b + 2)
                    for h in range(2):
                        free_T(before, h)
                        for n in range(4):
                            dst = psT[:, h, n * P:n * P + P]
                            col = 4 * h + n
                            nc.tensor.matmul(dst, rn[0][:, col:col + 1].broadcast_to([P, P]), ident_r[:, :],
                                             start=True, stop=False)
                            last = nc.tensor.matmul(dst, rn[1][:, col:col + 1].broadcast_to([P, P]), ident_r[:, :],
                                                    start=False, stop=True)
                        last.then_inc(rn_mm, 1)

                def body(b, head, tail, late, ahead):
                    if head:
                        mm_k(b, 0)
                        mm_q(b, 0)
                    if late:
                        spread_norms(b - 2, ("k", b - 1, 3) if tail else ("q", b - 2, 3))
                    if tail:
                        context(b - 1, 0)
                        tr_q(b - 1, 2, ("r", b - 2, 0) if late else ("k", b - 1, 3))
                        context(b - 1, 1)
                    if head:
                        shift_q(b, 0)
                        tr_k(b, 0, ("q", b - 1, 2) if tail else None)
                        mm_k(b, 1)
                    if tail:
                        fold(b - 1)
                    if head:
                        tr_c(b, ("k", b, 0))
                        mm_q(b, 1)
                        mm_k(b, 2)
                    if tail:
                        tr_q(b - 1, 3, ("c", b, 0) if head else ("q", b - 1, 2))
                    if head:
                        shift_q(b, 1)
                    if tail:
                        output(b - 1, 0, range(CH))
                    if head:
                        tr_k(b, 1, ("q", b - 1, 3) if tail else ("c", b, 0))
                        mm_k(b, 3)
                    if tail:
                        output(b - 1, 1, range(0, CH // 2))
                    if head:
                        tr_q(b, 0, ("k", b, 1))
                    if tail:
                        output(b - 1, 1, range(CH // 2, CH))
                    if head:
                        mm_q(b, 2)
                        tr_k(b, 2, ("q", b, 0))
                        shift_q(b, 2)
                    if tail:
                        square_norms(b - 1)
                    if head:
                        tr_q(b, 1, ("k", b, 2))
                        mm_q(b, 3)
                        tr_k(b, 3, ("q", b, 1))
                        shift_q(b, 3)

                run(pe, body)

        ffn_phase(nc, ident, gates, ps, stage, st_loaded, started, wait_apart, rsqrt_step, three_pass, A, B, Wr,
                  x2_dram, out)


def load_weight_rows(sp, t, A, B, stage, st_loaded, b_ready, w_T):
    E, R, D = A.shape
    P = 128
    EC, KC, ND = P // R, E * R // P, D // P
    slots = len(st_loaded)
    if t >= slots:
        before = t - slots
        if before < KC:
            sp.wait_ge(w_T, 2 * before + 2)
        else:
            k = before - KC
            sp.wait_ge(b_ready[k % 2], k // 2 + 1)
    slot = stage[:, t % slots, :]
    if t < KC:
        sp.dma_start(slot, A.rearrange("(k e) r d -> k (e r) d", e=EC)[t]).then_inc(st_loaded[t % slots], 16)
    else:
        sp.dma_start(slot.rearrange("p (e w) -> p e w", e=EC),
                     B.rearrange("(k e) (p d) r -> k p e (d r)", e=EC, d=ND)[t - KC]
                     ).then_inc(st_loaded[t % slots], 16)


def ffn_phase(nc, ident, gates, ps, stage, st_loaded, started, wait_apart, rsqrt_step, three_pass, A, B, Wr,
              x2_dram, out):
    f32 = mybir.dt.float32
    f32r = mybir.dt.float32r
    ALU = mybir.AluOpType
    ACT = mybir.ActivationFunctionType
    AX = mybir.AxisListType
    NB, T, D = out.shape
    E, R = A.shape[0], A.shape[1]
    KR = E * R
    P = 128
    DC = D // P
    KC = KR // P
    EC = E // KC
    SCALING = 32.0 / R
    LN_EPS = 1e-5
    NEWTON, NCH = 3, 11
    NEG = -3.0e38
    ND = D // P
    SLOTS = 4
    with ExitStack() as ph:
        def sb(name, shape, dt=f32):
            return ph.enter_context(nc.sbuf_tensor(name, shape, dt))

        def sem(name):
            return ph.enter_context(nc.semaphore(name))

        NSTG = len(st_loaded)
        b_stage = sb("b_stage", [P, 2, D])
        wr_stage = sb("wr_stage", [E, D])
        aT = [sb("aT_hi", [P, DC, KR], f32r), sb("aT_lo", [P, DC, KR], f32r)]
        bT = [sb("bT_hi", [P, KC, D], f32r), sb("bT_lo", [P, KC, D], f32r)]
        wrT = sb("wrT", [P, DC, E])
        gf = sb("gf", [P, 1])
        x2_own = sb("x2_own", [P, 2, D])
        x2b = [x2_own[:, 0, :], x2_own[:, 1, :], stage[:, 0, :], stage[:, 1, :]]
        res = b_stage
        y = sb("y", [P, D])
        yf = sb("yf", [P, DC, T])
        yT = [sb("yT_hi", [P, DC, T], f32r), sb("yT_lo", [P, DC, T], f32r)]
        hg = sb("hg", [P, KR])
        hT = [sb("hT_hi", [P, KC, T], f32r), sb("hT_lo", [P, KC, T], f32r)]
        bn = sb("bn2", [P, 2, 6])
        mv = sb("mv2", [P, 2])
        s1, y1, t1 = sb("s1", [P, 1]), sb("y1", [P, 1]), sb("t1", [P, 1])
        nb1 = sb("nb1", [P, 1])
        sc = sb("sc", [P, E])
        top8 = sb("top8", [P, 2, 8])
        rest = sb("rest", [P, 2, E])
        neg_top = sb("neg_top", [P, 1])
        ex = sb("ex", [P, E])
        gsel = sb("gsel", [P, E])
        gsum = sb("gsum", [P, 1])
        grec = sb("grec", [P, 1])
        gate = sb("gate", [P, E])

        dve_turns = sem("dve2_turns")
        wr_loaded, wr_T, wr_done = sem("wr_loaded"), sem("wr_T"), sem("wr_done")
        w_T, w_hi, w_lo, gf_done = sem("w2_T"), sem("w2_hi"), sem("w2_lo"), sem("gf_done")
        b_ready = [sem("b_ready0"), sem("b_ready1")]
        x2_loaded = [sem(f"x2_loaded{n}") for n in range(SLOTS)]
        out_stored = [sem("out_stored0"), sem("out_stored1")]
        stats_step, newton_step, nb_done, y_done = (
            sem("stats2_step"), sem("newton2_step"), sem("nb2_done"), sem("y_done"))
        y_T, y_full, y_hi, y_lo = sem("y_T"), sem("y_full"), sem("y_hi"), sem("y_lo")
        sc_mm, top_step, sc_exp = sem("sc_mm"), sem("top_step"), sem("sc_exp")
        h_mm, hg_done, h_T, h_hi, h_lo = (
            sem("h_mm"), sem("hg_done"), sem("h_T"), sem("h_hi"), sem("h_lo"))
        f_mm, res_done = sem("f_mm"), sem("res_done")
        psH, psF, psY, psG, psS = ps[:, 0:2, :], ps[:, 2:4, :], ps[:, 4:6, :], ps[:, 6, :], ps[:, 7, 0:E]
        TOP = 11

        def bank_of(u):
            return u % 4 if u < 2 * KC else (2, 3, 6)[(u - 2 * KC) % 3]

        def weight_part(part, t, h):
            bank = ps[:, bank_of(2 * t + h), :]
            if t < KC:
                return (aT[part][:, 4 * h:4 * h + 4, t * P:t * P + P], bank.rearrange("p (n r) -> p n r", r=P))
            dst = bT[part][:, t - KC, :].rearrange("p (q d) -> p q d", d=ND)[:, :, 4 * h:4 * h + 4]
            return dst, bank.rearrange("p (n q) -> p q n", q=P)

        def reorder(copy, k):
            return copy(b_stage[:, k % 2, :].rearrange("p (d e r) -> p e d r", e=EC, d=ND),
                        stage[:, (KC + k) % NSTG, :].rearrange("p (e d r) -> p e d r", e=EC, d=ND)
                        ).then_inc(b_ready[k % 2], 1)

        block = ph.enter_context(nc.Block())

        @block.sync
        def _(sp):
            def load(b, slot):
                sp.dma_start(x2b[slot],
                             x2_dram[bass.ds(b, 1)].rearrange("o p n -> (o p) n")).then_inc(x2_loaded[slot], 16)

            load(0, 0)
            sp.dma_start(wr_stage[:, :], Wr).then_inc(wr_loaded, 16)
            for t in range(NSTG, 2 * KC):
                load_weight_rows(sp, t, A, B, stage, st_loaded, b_ready, w_T)
                if t == NSTG + 1:
                    load(1, 1)
            for slot in (2, 3):
                k = KC - NSTG + slot - 2
                sp.wait_ge(b_ready[k % 2], k // 2 + 1)
                load(slot, slot)

            def group(i, last):
                for j in range(SLOTS):
                    b = SLOTS * i + j
                    sp.wait_ge(res_done, 2 * b + 2)
                    sp.dma_start(out[bass.ds(b, 1)].rearrange("o p n -> (o p) n"),
                                 res[:, j % 2, :]).then_inc(out_stored[j % 2], 16)
                    if not last:
                        load(b + SLOTS, j)

            with sp.Fori(0, NB // SLOTS - 1) as i:
                group(i, False)
            group(NB // SLOTS - 1, True)
            for half in range(2):
                sp.wait_ge(out_stored[half], 16 * (NB // 2))

        @block.gpsimd
        def _(pool):
            def lo_y(b):
                for h in range(2):
                    n = slice(4 * h, 4 * h + 4)
                    pool.wait_ge(y_hi, 2 * b + h + 1)
                    nc.gpsimd.tensor_tensor(yT[1][:, n, :], yf[:, n, :], yT[0][:, n, :].bitcast(f32),
                                            ALU.subtract).then_inc(y_lo, 1)

            for k in range(1, KC, 2):
                t = KC + k
                pool.wait_ge(st_loaded[t % NSTG], 16 * (t // NSTG + 1))
                if k >= 2:
                    pool.wait_ge(w_T, 2 * (t - 2) + 2)
                reorder(nc.gpsimd.tensor_copy, k)
                if k == 1:
                    lo_y(0)
            with pool.Fori(1, NB) as b:
                lo_y(b)

        @block.tensor
        def _(pe):
            def weight(t):
                if t < KC:
                    pe.wait_ge(st_loaded[t % NSTG], 16 * (t // NSTG + 1))
                else:
                    k = t - KC
                    pe.wait_ge(b_ready[k % 2], k // 2 + 1)
                for h in range(2):
                    u = 2 * t + h
                    ahead = 4 if t < KC else min(3, u - 2 * KC + 1)
                    if u >= ahead:
                        pe.wait_ge(w_lo, u - ahead + 1)
                    for n in range(4):
                        m = 4 * h + n
                        if t < KC:
                            src = stage[:, t % NSTG, m * P:m * P + P]
                        else:
                            src = b_stage[:, k % 2, m * P:m * P + P]
                        last = nc.tensor.transpose(ps[:, bank_of(u), n * P:n * P + P], src, ident[:, :])
                    last.then_inc(w_T, 1)

            def tr_y(b):
                pe.wait_ge(y_done, b + 1)
                for h in range(2):
                    if started(b):
                        pe.wait_ge(y_full, 2 * b - 2 + h + 1)
                    for n in range(4):
                        w = (4 * h + n) * P
                        last = nc.tensor.transpose(psY[:, h, n * P:n * P + P], y[:, w:w + P], ident[:, :])
                    last.then_inc(y_T, 1)

            def scores(b):
                pe.wait_ge(y_full, 2 * b + 2)
                if started(b):
                    pe.wait_ge(top_step, TOP * (b - 1) + 1)
                for m in range(DC):
                    last = nc.tensor.matmul(psS, yf[:, m, :], wrT[:, m, :], start=m == 0, stop=m == DC - 1)
                last.then_inc(sc_mm, 1)

            def up(b, g, chunks):
                if g == 0 and chunks[0] == 0:
                    pe.wait_ge(y_lo, 2 * b + 2)
                if started(b):
                    pe.wait_ge(hg_done, 2 * b - 2 + g + 1)
                v = slice(512 * g, 512 * g + 512)
                for m in chunks:
                    last = three_pass(psH[:, g, :], yT[0][:, m, :], yT[1][:, m, :], aT[0][:, m, v], aT[1][:, m, v],
                                      m == 0, m == DC - 1)
                if chunks[-1] == DC - 1:
                    last.then_inc(h_mm, 1)

            def tr_h(b, g):
                pe.wait_ge(hg_done, 2 * b + g + 1)
                if g == 1 or started(b):
                    pe.wait_ge(h_lo, 2 * b + g)
                else:
                    pe.wait_ge(w_lo, 4 * KC)
                for n in range(4):
                    w = (4 * g + n) * P
                    last = nc.tensor.transpose(psG[:, n * P:n * P + P], hg[:, w:w + P], ident[:, :])
                last.then_inc(h_T, 1)

            def down(b):
                for part in range(2):
                    pe.wait_ge(h_lo, 2 * b + part + 1)
                    for g in range(2):
                        if part == 0 and started(b):
                            pe.wait_ge(res_done, 2 * b - 2 + g + 1)
                        v = slice(512 * g, 512 * g + 512)
                        for m in range(KC // 2 * part, KC // 2 * (part + 1)):
                            last = three_pass(psF[:, g, :], hT[0][:, m, :], hT[1][:, m, :], bT[0][:, m, v],
                                              bT[1][:, m, v], m == 0, m == KC - 1)
                        if part == 1:
                            last.then_inc(f_mm, 1)

            def body(b, nxt):
                if started(b):
                    up(b, 0, range(DC))
                if nxt:
                    tr_y(b + 1)
                tr_h(b, 0)
                if started(b):
                    up(b, 1, range(DC))
                if nxt:
                    scores(b + 1)
                tr_h(b, 1)
                down(b)

            for t in range(KC):
                weight(t)
                if t == 1:
                    pe.wait_ge(wr_loaded, 16)
                    for m in range(DC):
                        last = nc.tensor.transpose(ps[:, 7, m * E:m * E + E], wr_stage[:, m * P:m * P + P],
                                                   ident[0:E, 0:E])
                    last.then_inc(wr_T, 1)
            tr_y(0)
            pe.wait_ge(wr_done, 1)
            scores(0)
            for k in range(KC):
                weight(KC + k)
                up(0, 2 * k // KC, range(2 * k % KC, 2 * k % KC + 2))
            body(0, True)
            with pe.Fori(1, NB - 1) as b:
                body(b, True)
            body(NB - 1, False)

        @block.scalar
        def _(act):
            nc.scalar.activation(gf[:, :], gates[:, 1:2], ACT.Copy, scale=SCALING).then_inc(gf_done, 1)

            def hi_weight(t):
                for h in range(2):
                    act.wait_ge(w_T, 2 * t + h + 1)
                    dst, src = weight_part(0, t, h)
                    nc.scalar.activation(dst, src, ACT.Copy).then_inc(w_hi, 1)

            def normalise(b, slot):
                act.wait_ge(nb_done, b + 1)
                if started(b):
                    act.wait_ge(y_T, 2 * b)
                nc.scalar.activation(y[:, :], x2b[slot], ACT.Identity, bias=nb1[:, 0:1],
                                     scale=y1[:, 0:1]).then_inc(y_done, 1)

            def full_y(b):
                if started(b):
                    act.wait_ge(sc_mm, b)
                    act.wait_ge(y_lo, 2 * b)
                for h in range(2):
                    act.wait_ge(y_T, 2 * b + h + 1)
                    nc.scalar.activation(yf[:, 4 * h:4 * h + 4, :],
                                         psY[:, h, :].rearrange("p (n c) -> p n c", c=P),
                                         ACT.Copy).then_inc(y_full, 1)

            def hi_y(b):
                act.wait_ge(y_full, 2 * b + 2)
                if started(b):
                    act.wait_ge(h_mm, 2 * b)
                for h in range(2):
                    n = slice(4 * h, 4 * h + 4)
                    nc.scalar.activation(yT[0][:, n, :], yf[:, n, :], ACT.Copy).then_inc(y_hi, 1)

            def hi_h(b, g):
                act.wait_ge(h_T, 2 * b + g + 1)
                nc.scalar.activation(hT[0][:, 4 * g:4 * g + 4, :], psG.rearrange("p (n c) -> p n c", c=P),
                                     ACT.Copy).then_inc(h_hi, 1)

            def exp_scores(b):
                act.wait_ge(top_step, TOP * b + 3)
                nc.scalar.activation(ex[:, :], sc[:, :], ACT.Exp, bias=neg_top[:, 0:1]).then_inc(sc_exp, 1)

            def body(b, slot, nxt, nxt2):
                if nxt:
                    full_y(b + 1)
                hi_h(b, 0)
                hi_h(b, 1)
                if nxt:
                    hi_y(b + 1)
                    exp_scores(b + 1)
                if nxt2:
                    normalise(b + 2, (slot + 2) % SLOTS)

            for t in range(KC):
                hi_weight(t)
                if t == 2:
                    act.wait_ge(wr_T, 1)
                    nc.scalar.activation(wrT[:, :, :].rearrange("p a b -> p (a b)"), ps[:, 7, :],
                                         ACT.Copy).then_inc(wr_done, 1)
                if t == 5:
                    normalise(0, 0)
            full_y(0)
            hi_y(0)
            hi_weight(KC)
            exp_scores(0)
            for k in range(1, KC):
                hi_weight(KC + k)
                if k == 4:
                    normalise(1, 1)
            for b in range(SLOTS):
                body(b, b, True, True)
            with act.Fori(1, NB // SLOTS - 1) as i:
                for j in range(SLOTS):
                    body(SLOTS * i + j, j, True, True)
            for j in range(SLOTS):
                body(NB - SLOTS + j, j, j < SLOTS - 1, j < SLOTS - 2)

        @block.vector
        def _(dve):
            def lo_weight(t):
                for h in range(2):
                    dve.wait_ge(w_hi, 2 * t + h + 1)
                    dst, src = weight_part(1, t, h)
                    hi, _ = weight_part(0, t, h)
                    nc.vector.tensor_tensor(dst, src, hi.bitcast(f32), ALU.subtract).then_inc(w_lo, 1)

            def reorder_even(k):
                t = KC + k
                dve.wait_ge(st_loaded[t % NSTG], 16 * (t // NSTG + 1))
                if k >= 2:
                    dve.wait_ge(w_T, 2 * (t - 2) + 2)
                reorder(nc.vector.tensor_copy, k)

            NS = 4

            def stats(b, slot, uses):
                dve.wait_ge(x2_loaded[slot], 16 * (uses + 1))
                for h in range(2):
                    nc.vector.bn_stats(bn[:, h, :], x2b[slot][:, 512 * h:512 * h + 512]).then_inc(stats_step, 1)
                wait_apart(dve, dve_turns, (stats_step, NS * b + 2), *([(y_done, b)] if started(b) else []))
                nc.vector.bn_aggr(mv[:, :], bn[:, :, :].rearrange("p a b -> p (a b)")).then_inc(stats_step, 1)
                dve.wait_ge(stats_step, NS * b + 3)
                nc.vector.tensor_scalar(s1[:, :], mv[:, 1:2], LN_EPS, None, ALU.add).then_inc(stats_step, 1)
                dve.wait_ge(stats_step, NS * b + 4)
                for k in range(NCH):
                    rsqrt_step(dve, k, y1[:, :], t1[:, :], s1[:, :], newton_step, NCH * b)
                dve.wait_ge(newton_step, NCH * (b + 1))
                nc.vector.scalar_tensor_tensor(nb1[:, :], mv[:, 0:1], -1.0, y1[:, :], ALU.mult,
                                               ALU.mult).then_inc(nb_done, 1)

            def route(b):
                step = [0]

                def link(ins, alone=False):
                    step[0] += 1
                    ins.then_inc(top_step, 1)
                    if alone:
                        wait_apart(dve, dve_turns, (top_step, TOP * b + step[0]))
                    else:
                        dve.wait_ge(top_step, TOP * b + step[0])

                dve.wait_ge(sc_mm, b + 1)
                link(nc.vector.tensor_copy(sc[:, :], psS), True)
                link(nc.vector.max(top8[:, 0, :], sc[:, :]))
                link(nc.vector.tensor_scalar(neg_top[:, :], top8[:, 0, 0:1], -1.0, None, ALU.mult), True)
                link(nc.vector.match_replace(rest[:, 0, :], top8[:, 0, :], sc[:, :], NEG), True)
                link(nc.vector.max(top8[:, 1, :], rest[:, 0, :]), True)
                link(nc.vector.match_replace(rest[:, 1, :], top8[:, 1, :], rest[:, 0, :], NEG))
                link(nc.vector.tensor_tensor(gsel[:, :], sc[:, :], rest[:, 1, :], ALU.not_equal))
                dve.wait_ge(sc_exp, b + 1)
                link(nc.vector.tensor_tensor(gsel[:, :], gsel[:, :], ex[:, :], ALU.mult))
                link(nc.vector.tensor_reduce(gsum[:, :], gsel[:, :], axis=AX.X, op=ALU.add))
                link(nc.vector.reciprocal(grec[:, :], gsum[:, :]))
                link(nc.vector.tensor_scalar(gate[:, :], gsel[:, :], grec[:, 0:1], None, ALU.mult))
                assert step[0] == TOP

            def gated(b, g):
                dve.wait_ge(h_mm, 2 * b + g + 1)
                if started(b):
                    dve.wait_ge(h_T, 2 * b - 1 + g)
                n = 512 // R
                nc.vector.tensor_tensor(hg[:, 512 * g:512 * g + 512].rearrange("p (e r) -> p e r", r=R),
                                        psH[:, g, :].rearrange("p (e r) -> p e r", r=R),
                                        gate[:, n * g:n * g + n].unsqueeze(2).broadcast_to([P, n, R]),
                                        ALU.mult).then_inc(hg_done, 1)

            def lo_h(b, g):
                dve.wait_ge(h_hi, 2 * b + g + 1)
                nc.vector.tensor_tensor(hT[1][:, 4 * g:4 * g + 4, :], psG.rearrange("p (n c) -> p n c", c=P),
                                        hT[0][:, 4 * g:4 * g + 4, :].bitcast(f32),
                                        ALU.subtract).then_inc(h_lo, 1)

            def result(b, slot, stores):
                for g in range(2):
                    dve.wait_ge(f_mm, 2 * b + g + 1)
                    if g == 0 and started(stores):
                        dve.wait_ge(out_stored[slot % 2], 16 * stores)
                    v = slice(512 * g, 512 * g + 512)
                    nc.vector.scalar_tensor_tensor(res[:, slot % 2, v], psF[:, g, :], gf[:, 0:1], x2b[slot][:, v],
                                                   ALU.mult, ALU.add).then_inc(res_done, 1)

            def body(i, slot, nxt, nxt2):
                b = SLOTS * i + slot
                gated(b, 0)
                lo_h(b, 0)
                if nxt2:
                    stats(b + 2, (slot + 2) % SLOTS, i + (slot + 2) // SLOTS)
                gated(b, 1)
                lo_h(b, 1)
                if nxt:
                    route(b + 1)
                result(b, slot, 2 * i + slot // 2)

            dve.wait_ge(gf_done, 1)
            for t in range(KC):
                lo_weight(t)
                if t == 3:
                    stats(0, 0, 0)
                if t == KC - 2:
                    reorder_even(0)
            route(0)
            for k in range(KC):
                if k % 2 == 1 and k + 1 < KC:
                    reorder_even(k + 1)
                lo_weight(KC + k)
                if k == 1:
                    stats(1, 1, 0)
            for j in range(SLOTS):
                body(0, j, True, True)
            with dve.Fori(1, NB // SLOTS - 1) as i:
                for j in range(SLOTS):
                    body(i, j, True, True)
            for j in range(SLOTS):
                body(NB // SLOTS - 1, j, j < SLOTS - 1, j < SLOTS - 2)


_INS = ["x", "ctx_4096", "g_xattn", "g_ffn", "L0_xattn_Wq", "L0_xattn_Wk", "L0_xattn_Wv", "L0_xattn_Wo",
        "L0_xattn_bo", "L0_xattn_g", "L0_ffn_A", "L0_ffn_B", "L0_ffn_Wr"]


def kernel(**inputs):
    import numpy as _np
    import concourse.bacc as _bacc
    from concourse import mybir as _mybir
    from concourse.bass_utils import run_bass_kernel_spmd as _run

    nc = _bacc.Bacc("TRN2", target_bir_lowering=False, num_devices=1)
    arrays, args = {}, []
    for name in _INS:
        a = _np.ascontiguousarray(inputs[name])
        arrays[f"in_{name}"] = a
        args.append(nc.dram_tensor(f"in_{name}", a.shape, _mybir.dt.from_np(a.dtype), kind="ExternalInput").ap())
    shape = tuple(inputs["x"].shape)
    scratch = nc.dram_tensor("x2_scratch", shape, _mybir.dt.float32, kind="Internal").ap()
    out = nc.dram_tensor("out_0", shape, _mybir.dt.float32, kind="ExternalOutput").ap()
    flamingo_layer(nc, *args, scratch, out)
    r = _run(nc, [arrays], core_ids=[0])
    return r.results[0]["out_0"]
```

```python
import concourse.bass as bass
from concourse import mybir
from contextlib import ExitStack
import math


def flamingo_layer(nc, x, ctx, g_xattn, g_ffn, Wq, Wk, Wv, Wo, bo, g, A, B, Wr, x2_dram, out):
    f32 = mybir.dt.float32
    f32r = mybir.dt.float32r
    i32 = mybir.dt.int32
    ALU = mybir.AluOpType
    ACT = mybir.ActivationFunctionType
    AX = mybir.AxisListType

    NB, C, N = x.shape
    HD = Wq.shape[0]
    DH = 64
    P = 128
    H = HD // DH
    CH = HD // P
    BK = N // P
    HF = N // 512
    E, R = A.shape[0], A.shape[1]
    KR = E * R
    LN_EPS = 1e-5
    MIN_SS = 1e-24
    MAGIC = 1597463007
    NEWTON = 3
    NCH = 2 + 3 * NEWTON
    NEG = -3.0e38

    def started(b):
        return not (isinstance(b, int) and b == 0)

    def wait_apart(eng, turns, *waits):
        for sem, value in waits:
            eng.wait_ge(sem, value)
        eng.sem_inc(turns, 1)

    def rsqrt_step(dve, k, y, t, s, sem, base):
        if k > 0:
            dve.wait_ge(sem, base + k)
        if k == 0:
            last = nc.vector.tensor_scalar(t.bitcast(i32), s.bitcast(i32), 1, None, ALU.logical_shift_right)
        elif k == 1:
            last = nc.vector.tensor_scalar(y.bitcast(i32), t.bitcast(i32), -1.0, float(MAGIC), ALU.mult, ALU.add)
        elif k % 3 == 2:
            last = nc.vector.tensor_tensor(t, y, s, ALU.mult)
        elif k % 3 == 0:
            last = nc.vector.scalar_tensor_tensor(t, t, -0.5, y, ALU.mult, ALU.mult)
        else:
            last = nc.vector.scalar_tensor_tensor(y, t, 1.5, y, ALU.add, ALU.mult)
        last.then_inc(sem, 1)

    def three_pass(psum, whi, wlo, mhi, mlo, start, stop):
        nc.tensor.matmul(psum, whi, mhi, start=start, stop=False)
        nc.tensor.matmul(psum, wlo, mhi, start=False, stop=False)
        return nc.tensor.matmul(psum, whi, mlo, start=False, stop=stop)

    outer = ExitStack()
    with outer:
        def const(name, shape, dt=f32):
            return outer.enter_context(nc.sbuf_tensor(name, shape, dt))

        def osem(name):
            return outer.enter_context(nc.semaphore(name))

        ident = const("ident", [P, P])
        ident_r = const("ident_r", [P, P], f32r)
        gates = const("gates", [P, 2])
        NSTG = 4
        stage = const("stage", [P, NSTG, A.shape[2]])
        st_loaded = [osem(f"st_loaded{n}") for n in range(NSTG)]
        EARLY = 2
        w_T = osem("w2_T")
        x2 = const("x2", [P, N])
        x2_stored = osem("x2_stored")
        x2_first = const("x2_first", [P, N])
        x2_loaded = [osem(f"x2_loaded{n}") for n in range(4)]
        ps = outer.enter_context(nc.psum_tensor("ps", [P, 8, 512], f32))
        psK = ps[:, 0:2, :]
        psQ = ps[:, 2:4, :]
        psT = ps[:, 4:6, :]
        psX = ps[:, 6:8, :]

        with ExitStack() as ph:
            def sb(name, shape, dt=f32):
                return ph.enter_context(nc.sbuf_tensor(name, shape, dt))

            def sem(name):
                return ph.enter_context(nc.semaphore(name))

            wstage = sb("wstage", [P, 4, CH, P])
            wk = [sb("wk_hi", [P, HD], f32r), sb("wk_lo", [P, HD], f32r)]
            wq = [sb("wq_hi", [P, HD], f32r), sb("wq_lo", [P, HD], f32r)]
            woT = sb("woT", [P, CH, P])
            wvo = [sb("wvo_hi", [P, CH, 2 * P], f32r), sb("wvo_lo", [P, CH, 2 * P], f32r)]
            g_raw = sb("g_raw", [P, 4])
            gcol = sb("gcol", [P, 1])
            gbo = sb("gbo", [P, 1])
            ones = sb("ones", [P, 1])
            ctx_in = sb("ctx_in", [P, N])
            x_in = sb("x_in", [P, N])
            x_res = sb("x_res", [P, N])
            cx = [sb("ctx_hi", [P, N], f32r), sb("ctx_lo", [P, N], f32r)]
            xn = sb("xn", [P, N])
            xs = [sb("xn_hi", [P, N], f32r), sb("xn_lo", [P, N], f32r)]
            cT = [sb("ctxT_hi", [P, BK, C], f32r), sb("ctxT_lo", [P, BK, C], f32r)]
            ek = sb("ek", [P, 2, N])
            ekT = [sb("ekT_hi", [P, BK, HD], f32r), sb("ekT_lo", [P, BK, HD], f32r)]
            kmax = sb("kmax", [P, CH])
            ksum = sb("ksum", [P, CH])
            krec = sb("krec", [P, CH])
            qe = sb("qe", [P, 4, 2 * HD])
            qmax = sb("qmax", [P, 2, 2 * H], f32r)
            qhalf = sb("qhalf", [P, 2, 2 * H * DH // 2])
            qsum = sb("qsum", [P, 4, 2 * H])
            qrec = sb("qrec", [P, 4, 2 * H])
            qT = [sb("qT_hi", [P, CH, N], f32r), sb("qT_lo", [P, CH, N], f32r)]
            kc = [sb("kc_hi", [P, HD], f32r), sb("kc_lo", [P, HD], f32r)]
            mt = sb("mt", [P, CH, P])
            mts = [sb("mt_hi", [P, CH, P], f32r), sb("mt_lo", [P, CH, P], f32r)]
            osb = sb("osb", [P, N])
            osq = sb("osq", [P, N])
            usb = sb("usb", [P, N])
            bn = sb("bn", [P, HF, 6])
            mv = sb("mv", [P, 2])
            root_s, root_y, root_t = sb("root_s", [P, BK + 1]), sb("root_y", [P, BK + 1]), sb("root_t", [P, BK + 1])
            rstd = root_y[:, BK:BK + 1]
            nbias = sb("nbias", [P, 1])

            dve_turns, sp_turns = sem("dve_turns"), sem("sp_turns")
            wk_loaded, wq_loaded, wvo_loaded, g_loaded = (
                sem("wk_loaded"), sem("wq_loaded"), sem("wvo_loaded"), sem("g_loaded"))
            id_ready, ones_ready = sem("id_ready"), sem("ones_ready")
            wT_done, w_hi, w_lo = sem("wT_done"), sem("w_hi"), sem("w_lo")
            fold_done, fold_hi, fold_lo = sem("fold_done"), sem("fold_hi"), sem("fold_lo")
            tanh_done, gcol_done = sem("tanh_done"), sem("gcol_done")
            ctx_loaded, x_loaded, xres_loaded = sem("ctx_loaded"), sem("x_loaded"), sem("xres_loaded")
            ctx_hi, ctx_lo, xn_hi, xn_lo = sem("ctx_hi"), sem("ctx_lo"), sem("xn_hi"), sem("xn_lo")
            stats_step, root_step, nbias_done, xn_done = (
                sem("stats_step"), sem("root_step"), sem("nbias_done"), sem("xn_done"))
            k_mm, k_max, k_exp, k_T, k_hi, k_lo, k_rec = (
                sem("k_mm"), sem("k_max"), sem("k_exp"), sem("k_T"), sem("k_hi"), sem("k_lo"),
                sem("k_rec"))
            q_mm, q_max, q_shift, q_exp, q_sum, q_rec, q_norm, q_T, q_hi, q_lo = (
                sem("q_mm"), sem("q_max"), sem("q_shift"), sem("q_exp"), sem("q_sum"),
                sem("q_rec"), sem("q_norm"), sem("q_T"), sem("q_hi"), sem("q_lo"))
            q_half, o_sq = sem("q_half"), sem("o_sq")
            c_T, c_hi, c_lo = sem("c_T"), sem("c_hi"), sem("c_lo")
            kc_mm, kc_hi, kc_lo = sem("kc_mm"), sem("kc_hi"), sem("kc_lo")
            m_mm, m_scaled, m_hi, m_lo = sem("m_mm"), sem("m_scaled"), sem("m_hi"), sem("m_lo")
            o_mm, o_out, ss_mm, ss_read, rn_mm, rn_out, u_done, x2_done = (
                sem("o_mm"), sem("o_out"), sem("ss_mm"), sem("ss_read"), sem("rn_mm"), sem("rn_out"),
                sem("u_done"), sem("x2_done"))

            def run(eng, body):
                body(0, head=True, tail=False, late=False, ahead=True)
                body(1, head=True, tail=True, late=False, ahead=True)
                with eng.Fori(2, NB - 1) as b:
                    body(b, head=True, tail=True, late=True, ahead=True)
                body(NB - 1, head=True, tail=True, late=True, ahead=False)
                body(NB, head=False, tail=True, late=True, ahead=False)
                body(NB + 1, head=False, tail=False, late=True, ahead=False)

            block = ph.enter_context(nc.Block())

            @block.sync
            def _(sp):
                def load(dst, src, b, s):
                    sp.dma_start(dst, src[bass.ds(b, 1)].rearrange("o p n -> (o p) n")).then_inc(s, 16)

                load(ctx_in[:, :], ctx, 0, ctx_loaded)
                load(x_in[:, :], x, 0, x_loaded)
                load(x_res[:, :], x, 0, xres_loaded)
                sp.wait_ge(xn_done, 1)
                load(x_in[:, :], x, 1, x_loaded)
                for t in range(NSTG):
                    load_weight_rows(sp, t, A, B, stage, st_loaded, None, None)

                def body(b, head, tail, late, ahead):
                    if ahead:
                        wait_apart(sp, sp_turns, (c_T, 2 * b + 2))
                        wait_apart(sp, sp_turns, (ctx_lo, 2 * b + 2))
                        load(ctx_in[:, :], ctx, b + 1, ctx_loaded)
                        if not (isinstance(b, int) and b == NB - 2):
                            wait_apart(sp, sp_turns, (xn_done, b + 2))
                            load(x_in[:, :], x, b + 2, x_loaded)
                    if late:
                        wait_apart(sp, sp_turns, (x2_done, b - 1))
                        sp.dma_start(x2_dram[bass.ds(b - 2, 1)].rearrange("o p n -> (o p) n"),
                                     x2[:, :]).then_inc(x2_stored, 16)
                        if tail:
                            load(x_res[:, :], x, b - 1, xres_loaded)

                body(0, head=True, tail=False, late=False, ahead=True)
                body(1, head=True, tail=True, late=False, ahead=True)
                with sp.Fori(2, NB - 2) as b:
                    body(b, head=True, tail=True, late=True, ahead=True)
                body(NB - 2, head=True, tail=True, late=True, ahead=True)
                body(NB - 1, head=True, tail=True, late=True, ahead=False)
                body(NB, head=False, tail=True, late=True, ahead=False)
                sp.wait_ge(x2_stored, 16 * 2)
                sp.dma_start(x2_first[:, :], x2_dram[0]).then_inc(x2_loaded[0], 16)
                for t in range(NSTG, NSTG + EARLY):
                    load_weight_rows(sp, t, A, B, stage, st_loaded, None, w_T)
                body(NB + 1, head=False, tail=False, late=True, ahead=False)

            @block.gpsimd
            def _(pool):
                nc.gpsimd.memset(ident[:, :], 0.0).then_inc(id_ready, 1)
                pool.wait_ge(id_ready, 1)
                nc.gpsimd.affine_select(out=ident[:, :], in_=ident[:, :], compare_op=ALU.not_equal,
                                        fill=1.0, base=0, pattern=[[-1, P]],
                                        channel_multiplier=1).then_inc(id_ready, 1)
                pool.wait_ge(id_ready, 2)
                nc.gpsimd.tensor_scalar(ident_r[:, :], ident[:, :], 1.0, 0.0, ALU.mult,
                                        ALU.add).then_inc(id_ready, 1)
                nc.gpsimd.memset(ones[:, :], 1.0).then_inc(ones_ready, 1)

                def lo_ctx(b, h):
                    pool.wait_ge(ctx_hi, 2 * b + h + 1)
                    v = slice(512 * h, 512 * h + 512)
                    nc.gpsimd.tensor_tensor(cx[1][:, v], ctx_in[:, v], cx[0][:, v].bitcast(f32),
                                            ALU.subtract).then_inc(ctx_lo, 1)

                def lo_xn(b, h):
                    pool.wait_ge(xn_hi, 2 * b + h + 1)
                    v = slice(512 * h, 512 * h + 512)
                    nc.gpsimd.tensor_tensor(xs[1][:, v], xn[:, v], xs[0][:, v].bitcast(f32),
                                            ALU.subtract).then_inc(xn_lo, 1)

                def halve(b, p):
                    pool.wait_ge(q_exp, 4 * b + p + 1)
                    if p > 1 or started(b):
                        pool.wait_ge(q_sum, 4 * b + p - 1)
                    v = qe[:, p, :].rearrange("p (h d) -> p h d", d=DH)
                    nc.gpsimd.tensor_tensor(qhalf[:, p % 2, :].rearrange("p (h d) -> p h d", d=DH // 2),
                                            v[:, :, 0:DH // 2], v[:, :, DH // 2:DH], ALU.add).then_inc(q_half, 1)

                def normalise(b, p):
                    pool.wait_ge(q_rec, 4 * b + p + 1)
                    v = qe[:, p, :].rearrange("p (h d) -> p h d", d=DH)
                    w = qrec[:, p, :].unsqueeze(2).broadcast_to([P, 2 * H, DH])
                    nc.gpsimd.tensor_tensor(v, v, w, ALU.mult).then_inc(q_norm, 1)

                def gated(b, h):
                    pool.wait_ge(rn_out, 2 * b + h + 1)
                    v = slice(512 * h, 512 * h + 512)
                    nc.gpsimd.tensor_tensor(usb[:, v], osb[:, v], usb[:, v], ALU.mult).then_inc(u_done, 1)

                def finish(b):
                    pool.wait_ge(xres_loaded, 16 * (b + 1))
                    if started(b):
                        pool.wait_ge(x2_stored, 16 * b)
                    pool.wait_ge(u_done, 2 * b + 2)
                    nc.gpsimd.tensor_tensor(x2[:, :], usb[:, :], x_res[:, :], ALU.add).then_inc(x2_done, 1)

                def body(b, head, tail, late, ahead):
                    if tail:
                        halve(b - 1, 3)
                    if head:
                        lo_xn(b, 1)
                    if tail and not head:
                        normalise(b - 1, 2)
                        normalise(b - 1, 3)
                    if late and tail:
                        gated(b - 2, 0)
                        gated(b - 2, 1)
                    if tail and head:
                        normalise(b - 1, 2)
                        normalise(b - 1, 3)
                    if head:
                        halve(b, 0)
                    if tail:
                        pool.wait_ge(m_hi, b)
                        nc.gpsimd.tensor_tensor(mts[1][:, :, :], mt[:, :, :], mts[0][:, :, :].bitcast(f32),
                                                ALU.subtract).then_inc(m_lo, 1)
                    if late and tail:
                        finish(b - 2)
                    if head:
                        normalise(b, 0)
                    if ahead:
                        lo_ctx(b + 1, 0)
                        lo_ctx(b + 1, 1)
                    if head:
                        halve(b, 1)
                        normalise(b, 1)
                    if ahead:
                        lo_xn(b + 1, 0)
                    if head:
                        halve(b, 2)

                lo_ctx(0, 0)
                lo_ctx(0, 1)
                lo_xn(0, 0)
                run(pool, body)

            @block.scalar
            def _(act):
                act.dma_start(wstage[:, 0, :, :], Wk.rearrange("(j p) c -> p j c", p=P)).then_inc(wk_loaded, 16)
                act.dma_start(wstage[:, 1, :, :], Wq.rearrange("(j p) c -> p j c", p=P)).then_inc(wq_loaded, 16)
                act.dma_start(wstage[:, 2, :, :], Wv.rearrange("(j p) c -> p j c", p=P)).then_inc(wvo_loaded, 16)
                act.dma_start(wstage[:, 3, :, :], Wo.rearrange("o (j c) -> o j c", c=P)).then_inc(wvo_loaded, 16)
                act.dma_start(g_raw[:, 0:1], g_xattn.rearrange("(a n) -> a n", a=1).broadcast_to([P, 1])).then_inc(g_loaded, 16)
                act.dma_start(g_raw[:, 1:2], g_ffn.rearrange("(a n) -> a n", a=1).broadcast_to([P, 1])).then_inc(g_loaded, 16)
                act.dma_start(g_raw[:, 2:3], g[0]).then_inc(g_loaded, 16)
                act.dma_start(g_raw[:, 3:4], bo.rearrange("(p a) -> p a", a=1)).then_inc(g_loaded, 16)
                bo_col = g_raw[:, 3:4]

                def norm_x(b):
                    act.wait_ge(nbias_done, b + 1)
                    nc.scalar.activation(xn[:, :], x_in[:, :], ACT.Identity, bias=nbias[:, 0:1],
                                         scale=rstd).then_inc(xn_done, 1)

                def hi_ctx(b, h):
                    act.wait_ge(ctx_loaded, 16 * (b + 1))
                    if started(b):
                        act.wait_ge(k_mm, 4 * b)
                    v = slice(512 * h, 512 * h + 512)
                    nc.scalar.activation(cx[0][:, v], ctx_in[:, v], ACT.Copy).then_inc(ctx_hi, 1)

                def hi_xn(b, h):
                    if started(b):
                        act.wait_ge(q_mm, 4 * b - 4 + 2 * h + 2)
                    act.wait_ge(xn_done, b + 1)
                    v = slice(512 * h, 512 * h + 512)
                    nc.scalar.activation(xs[0][:, v], xn[:, v], ACT.Copy).then_inc(xn_hi, 1)

                hi_ctx(0, 0)
                hi_ctx(0, 1)
                act.wait_ge(wT_done, 1)
                nc.scalar.activation(wk[0][:, :], psT[:, 0, :], ACT.Copy).then_inc(w_hi, 1)
                act.wait_ge(wT_done, 2)
                nc.scalar.activation(wq[0][:, :], psT[:, 1, :], ACT.Copy).then_inc(w_hi, 1)
                norm_x(0)
                hi_xn(0, 0)

                def exp_k(b, j):
                    act.wait_ge(k_max, 4 * b + j + 1)
                    if j == 0 and started(b):
                        act.wait_ge(k_rec, b)
                    if j >= 2 or started(b):
                        act.wait_ge(k_T, 8 * b + 2 * j - 2)
                    nc.scalar.activation(ek[:, j % 2, :].rearrange("p (a n) -> p a n", a=HF), psK,
                                         ACT.Exp, bias=kmax[:, j:j + 1],
                                         accum_out=ksum[:, j:j + 1]).then_inc(k_exp, 1)

                def exp_q(b, p):
                    act.wait_ge(q_shift, 4 * b + p + 1)
                    if started(b):
                        act.wait_ge(q_T, 8 * b + 2 * p - 6)
                    nc.scalar.activation(qe[:, p, :].rearrange("p (a n) -> p a n", a=2), psQ,
                                         ACT.Exp).then_inc(q_exp, 1)

                def hi_q(b, p):
                    for h in range(2):
                        act.wait_ge(q_T, 8 * b + 2 * p + h + 1)
                        nb = 2 * p + h
                        nc.scalar.activation(qT[0][:, :, nb * P:nb * P + P],
                                             psT[:, h, :].rearrange("p (j n) -> p j n", n=P),
                                             ACT.Copy).then_inc(q_hi, 1)

                def hi_k(b, j):
                    for h in range(2):
                        act.wait_ge(k_T, 8 * b + 2 * j + h + 1)
                        nc.scalar.activation(ekT[0][:, 4 * h:4 * h + 4, j * P:j * P + P],
                                             psT[:, h, :].rearrange("p (n d) -> p n d", d=P),
                                             ACT.Copy).then_inc(k_hi, 1)

                def out_o(b, h):
                    if h == 0 and not started(b):
                        act.wait_ge(gcol_done, 2)
                    act.wait_ge(o_mm, 2 * b + h + 1)
                    v = slice(512 * h, 512 * h + 512)
                    nc.scalar.activation(osq[:, v], psX[:, h, :], ACT.Square, bias=bo_col).then_inc(o_sq, 1)
                    nc.scalar.activation(osb[:, v], psX[:, h, :], ACT.Identity, bias=gbo[:, 0:1],
                                         scale=gcol[:, 0:1]).then_inc(o_out, 1)

                def hi_c(b, h):
                    act.wait_ge(c_T, 2 * b + h + 1)
                    nc.scalar.activation(cT[0][:, 4 * h:4 * h + 4, :], psT[:, h, :].rearrange("p (n c) -> p n c", c=P),
                                         ACT.Copy).then_inc(c_hi, 1)

                def body(b, head, tail, late, ahead):
                    if tail:
                        exp_q(b - 1, 3)
                    if not started(b):
                        hi_c(b, 0)
                        hi_c(b, 1)
                    if head:
                        hi_xn(b, 1)
                    if late and tail:
                        for h in range(2):
                            act.wait_ge(rn_mm, 2 * b - 4 + h + 1)
                            nc.scalar.activation(usb[:, 512 * h:512 * h + 512], psT[:, h, :],
                                                 ACT.Copy).then_inc(rn_out, 1)
                    if tail:
                        act.wait_ge(kc_mm, b)
                        nc.scalar.activation(kc[0][:, :], psX[:, 0, :], ACT.Copy).then_inc(kc_hi, 1)
                    if head:
                        if started(b):
                            hi_c(b, 0)
                            hi_c(b, 1)
                        else:
                            act.wait_ge(g_loaded, 64)
                            nc.scalar.activation(gates[:, :], g_raw[:, 0:2], ACT.Tanh).then_inc(tanh_done, 1)
                            act.wait_ge(wT_done, 3)
                            nc.scalar.activation(woT[:, :, :].rearrange("p a b -> p (a b)"), psX[:, 0, :],
                                                 ACT.Copy).then_inc(w_hi, 1)
                        exp_q(b, 0)
                        exp_k(b, 1)
                    if tail:
                        hi_q(b - 1, 1)
                        if not head:
                            hi_q(b - 1, 2)
                        act.wait_ge(m_scaled, 2 * b)
                        nc.scalar.activation(mts[0][:, :, :], mt[:, :, :], ACT.Copy).then_inc(m_hi, 1)
                    if ahead:
                        act.wait_ge(xn_lo, 2 * b + 2)
                        norm_x(b + 1)
                    if head:
                        hi_k(b, 0)
                        exp_k(b, 2)
                        exp_q(b, 1)
                    if tail and head:
                        hi_q(b - 1, 2)
                    if ahead:
                        hi_ctx(b + 1, 0)
                        hi_ctx(b + 1, 1)
                    if head:
                        if not started(b):
                            act.wait_ge(fold_done, 1)
                            for par in range(2):
                                nc.scalar.activation(wvo[0][:, :, par * P:par * P + P],
                                                     psX[:, par, :].rearrange("p (j o) -> p j o", o=P),
                                                     ACT.Copy, scale=DH ** -0.5).then_inc(fold_hi, 1)
                        hi_k(b, 1)
                        exp_k(b, 3)
                    if tail:
                        hi_q(b - 1, 3)
                        out_o(b - 1, 0)
                    if head:
                        exp_q(b, 2)
                    if ahead:
                        hi_xn(b + 1, 0)
                    if head:
                        hi_k(b, 2)
                    if ahead:
                        exp_k(b + 1, 0)
                    if head:
                        hi_q(b, 0)
                    if tail:
                        out_o(b - 1, 1)
                    if head:
                        hi_k(b, 3)

                exp_k(0, 0)
                run(act, body)

            @block.vector
            def _(dve):
                NS = HF + 2

                def stats(b):
                    dve.wait_ge(x_loaded, 16 * (b + 1))
                    for h in range(HF):
                        nc.vector.bn_stats(bn[:, h, :], x_in[:, 512 * h:512 * h + 512]).then_inc(stats_step, 1)
                    wait_apart(dve, dve_turns, (stats_step, NS * b + HF), *([(nbias_done, b)] if started(b) else []))
                    nc.vector.bn_aggr(mv[:, :], bn[:, :, :].rearrange("p a b -> p (a b)")).then_inc(stats_step, 1)
                    dve.wait_ge(stats_step, NS * b + HF + 1)
                    nc.vector.tensor_scalar(root_s[:, BK:BK + 1], mv[:, 1:2], LN_EPS, None, ALU.add).then_inc(stats_step, 1)

                def roots(run, norms, var):
                    cols = slice(0 if norms is not None else BK, BK + 1 if var is not None else BK)
                    if norms is not None:
                        dve.wait_ge(ss_mm, norms + 1)
                        nc.vector.tensor_scalar(root_s[:, 0:BK], psX[:, 1, 0:BK], MIN_SS, None,
                                                ALU.max).then_inc(ss_read, 1)
                        dve.wait_ge(ss_read, norms + 1)
                    if var is not None:
                        dve.wait_ge(stats_step, NS * (var + 1))
                    for k in range(NCH):
                        if k == 1 and var is not None and started(var):
                            dve.wait_ge(xn_done, var)
                        rsqrt_step(dve, k, root_y[:, cols], root_t[:, cols], root_s[:, cols], root_step, NCH * run)
                    if var is not None:
                        dve.wait_ge(root_step, NCH * (run + 1))
                        nc.vector.scalar_tensor_tensor(nbias[:, :], mv[:, 0:1], -1.0, rstd, ALU.mult,
                                                       ALU.mult).then_inc(nbias_done, 1)

                stats(0)
                for n, w in enumerate((wk, wq)):
                    if n == 1:
                        roots(0, None, 0)
                    dve.wait_ge(w_hi, n + 1)
                    nc.vector.tensor_tensor(w[1][:, :], psT[:, n, :], w[0][:, :].bitcast(f32),
                                            ALU.subtract).then_inc(w_lo, 1)

                def max_k(b, j):
                    dve.wait_ge(k_mm, 4 * b + j + 1)
                    nc.vector.tensor_reduce(kmax[:, j:j + 1], psK, axis=AX.XY, op=ALU.max,
                                            negate=True).then_inc(k_max, 1)

                def max_q(b, p):
                    dve.wait_ge(q_mm, 4 * b + p + 1)
                    nc.vector.tensor_reduce(qmax[:, p % 2, :], psQ.rearrange("p a (h d) -> p (a h) d", d=DH),
                                            axis=AX.X, op=ALU.max, negate=True).then_inc(q_max, 1)

                def sum_q(b, p):
                    dve.wait_ge(q_half, 4 * b + p + 1)
                    nc.vector.tensor_reduce(qsum[:, p, :], qhalf[:, p % 2, :].rearrange("p (h d) -> p h d", d=DH // 2),
                                            axis=AX.X, op=ALU.add).then_inc(q_sum, 1)
                    dve.wait_ge(q_sum, 4 * b + p + 1)
                    nc.vector.reciprocal(qrec[:, p, :], qsum[:, p, :]).then_inc(q_rec, 1)

                def lo_q(b, p, h):
                    dve.wait_ge(q_hi, 8 * b + 2 * p + h + 1)
                    v = slice((2 * p + h) * P, (2 * p + h + 1) * P)
                    nc.vector.tensor_tensor(qT[1][:, :, v], psT[:, h, :].rearrange("p (j n) -> p j n", n=P),
                                            qT[0][:, :, v].bitcast(f32), ALU.subtract).then_inc(q_lo, 1)

                def lo_k(b, j, h):
                    dve.wait_ge(k_hi, 8 * b + 2 * j + h + 1)
                    n, w = slice(4 * h, 4 * h + 4), slice(j * P, j * P + P)
                    nc.vector.tensor_tensor(ekT[1][:, n, w], psT[:, h, :].rearrange("p (n d) -> p n d", d=P),
                                            ekT[0][:, n, w].bitcast(f32), ALU.subtract).then_inc(k_lo, 1)

                def lo_c(b, h):
                    dve.wait_ge(c_hi, 2 * b + h + 1)
                    n = slice(4 * h, 4 * h + 4)
                    nc.vector.tensor_tensor(cT[1][:, n, :], psT[:, h, :].rearrange("p (n c) -> p n c", c=P),
                                            cT[0][:, n, :].bitcast(f32), ALU.subtract).then_inc(c_lo, 1)

                def finish_last(b):
                    halves = [slice(512 * h, 512 * h + 512) for h in range(2)]
                    dve.wait_ge(x2_stored, 16 * b)
                    for h, v in enumerate(halves):
                        dve.wait_ge(rn_mm, 2 * b + h + 1)
                        nc.vector.tensor_tensor(usb[:, v], osb[:, v], psT[:, h, :], ALU.mult).then_inc(u_done, 1)
                    dve.wait_ge(xres_loaded, 16 * (b + 1))
                    for h, v in enumerate(halves):
                        dve.wait_ge(u_done, 2 * b + h + 1)
                        last = nc.vector.tensor_tensor(x2[:, v], usb[:, v], x_res[:, v], ALU.add)
                    last.then_inc(x2_done, 1)

                def scale_m(b, par):
                    dve.wait_ge(m_mm, b + 1)
                    dve.wait_ge(k_rec, b + 1)
                    v = psX.rearrange("p a (c w) -> p (a c) w", w=2 * P)
                    r = slice(DH * par, DH * par + DH)
                    nc.vector.tensor_tensor(mt[r, :, :], v[r, :, par * P:par * P + P],
                                            krec[r, :].unsqueeze(2).broadcast_to([DH, CH, P]),
                                            ALU.mult).then_inc(m_scaled, 1)

                def body(b, head, tail, late, ahead):
                    if not started(b):
                        lo_c(b, 0)
                        lo_c(b, 1)
                        max_q(b, 0)
                        max_k(b, 1)
                    if ahead:
                        stats(b + 1)
                    if late or ahead:
                        roots(b + 1, b - 2 if late else None, b + 1 if ahead else None)
                    if late and not tail:
                        finish_last(b - 2)
                    if tail:
                        sum_q(b - 1, 2)
                        sum_q(b - 1, 3)
                    if head and started(b):
                        max_q(b, 0)
                    if tail:
                        dve.wait_ge(kc_hi, b)
                        nc.vector.tensor_tensor(kc[1][:, :], psX[:, 0, :], kc[0][:, :].bitcast(f32),
                                                ALU.subtract).then_inc(kc_lo, 1)
                    if head and started(b):
                        lo_c(b, 0)
                        lo_c(b, 1)
                        max_k(b, 1)
                    if tail and not head:
                        lo_q(b - 1, 1, 0)
                        lo_q(b - 1, 1, 1)
                    if tail:
                        scale_m(b - 1, 0)
                        scale_m(b - 1, 1)
                    if tail and head:
                        lo_q(b - 1, 1, 0)
                        lo_q(b - 1, 1, 1)
                    if head:
                        max_q(b, 1)
                        max_k(b, 2)
                        lo_k(b, 0, 0)
                        lo_k(b, 0, 1)
                        sum_q(b, 0)
                    if tail:
                        lo_q(b - 1, 2, 0)
                        lo_q(b - 1, 2, 1)
                    if head:
                        max_k(b, 3)
                        max_q(b, 2)
                        lo_k(b, 1, 0)
                        lo_k(b, 1, 1)
                        if not started(b):
                            dve.wait_ge(tanh_done, 1)
                            nc.vector.scalar_tensor_tensor(gcol[:, :], g_raw[:, 2:3], math.sqrt(C), gates[:, 0:1],
                                                           ALU.mult, ALU.mult).then_inc(gcol_done, 1)
                            dve.wait_ge(gcol_done, 1)
                            nc.vector.tensor_tensor(gbo[:, :], gcol[:, :], g_raw[:, 3:4],
                                                    ALU.mult).then_inc(gcol_done, 1)
                            dve.wait_ge(fold_hi, 2)
                            for par in range(2):
                                nc.vector.scalar_tensor_tensor(wvo[1][:, :, par * P:par * P + P],
                                                               psX[:, par, :].rearrange("p (j o) -> p j o", o=P),
                                                               DH ** -0.5,
                                                               wvo[0][:, :, par * P:par * P + P].bitcast(f32),
                                                               ALU.mult, ALU.subtract).then_inc(fold_lo, 1)
                    if tail:
                        lo_q(b - 1, 3, 0)
                        lo_q(b - 1, 3, 1)
                    if head:
                        dve.wait_ge(k_exp, 4 * b + 4)
                        nc.vector.reciprocal(krec[:, :], ksum[:, :]).then_inc(k_rec, 1)
                    if ahead:
                        max_k(b + 1, 0)
                    if head:
                        sum_q(b, 1)
                        lo_k(b, 2, 0)
                        lo_k(b, 2, 1)
                        lo_q(b, 0, 0)
                        lo_q(b, 0, 1)
                        max_q(b, 3)
                        lo_k(b, 3, 0)
                        lo_k(b, 3, 1)

                max_k(0, 0)
                run(dve, body)

            @block.tensor
            def _(pe):
                pe.wait_ge(id_ready, 3)
                for n, loaded in ((0, wk_loaded), (1, wq_loaded)):
                    pe.wait_ge(loaded, 16)
                    for j in range(CH):
                        last = nc.tensor.transpose(psT[:, n, j * P:j * P + P], wstage[:, n, j, :], ident[:, :])
                    last.then_inc(wT_done, 1)

                def transpose_wo():
                    pe.wait_ge(wvo_loaded, 32)
                    for j in range(CH):
                        last = nc.tensor.transpose(psX[:, 0, j * P:j * P + P], wstage[:, 3, j, :], ident[:, :])
                    last.then_inc(wT_done, 1)

                def fold_weights():
                    pe.wait_ge(w_hi, 3)
                    for par in range(2):
                        r = slice(DH * par, DH * par + DH)
                        for j in range(CH):
                            last = nc.tensor.matmul(psX[:, par, j * P:j * P + P], wstage[r, 2, j, :],
                                                    woT[r, j, :], start=True, stop=True)
                    last.then_inc(fold_done, 1)

                def free_T(task, h):
                    if task is None:
                        return
                    kind, b, n = task
                    if kind == "c":
                        pe.wait_ge(c_lo, 2 * b + h + 1)
                    if kind == "k":
                        pe.wait_ge(k_lo, 8 * b + 2 * n + h + 1)
                    if kind == "q":
                        pe.wait_ge(q_lo, 8 * b + 2 * n + h + 1)
                    if kind == "r":
                        pe.wait_ge(rn_out, 2 * b + h + 1)

                def mm_k(b, j):
                    if j > 0:
                        pe.wait_ge(k_exp, 4 * b + j)
                    elif started(b):
                        pe.wait_ge(k_exp, 4 * b)
                    for h in range(HF):
                        if j == 0:
                            pe.wait_ge(ctx_lo, 2 * b + h + 1)
                        v = slice(512 * h, 512 * h + 512)
                        w = slice(P * j, P * j + P)
                        last = three_pass(psK[:, h, :], wk[0][:, w], wk[1][:, w], cx[0][:, v], cx[1][:, v],
                                          True, True)
                    last.then_inc(k_mm, 1)

                def mm_q(b, p):
                    if p % 2 == 0:
                        pe.wait_ge(xn_lo, 2 * b + p // 2 + 1)
                    if p > 0:
                        pe.wait_ge(q_exp, 4 * b + p)
                    elif started(b):
                        pe.wait_ge(q_exp, 4 * b)
                    for h in range(2):
                        w = slice(P * (2 * p + h), P * (2 * p + h) + P)
                        last = three_pass(psQ[:, h, :], xs[0][:, w], xs[1][:, w], wq[0][:, :], wq[1][:, :],
                                          True, True)
                    last.then_inc(q_mm, 1)

                def shift_q(b, p):
                    pe.wait_ge(q_max, 4 * b + p + 1)
                    for h in range(2):
                        m = qmax[:, p % 2, h * H:h * H + H].unsqueeze(2).broadcast_to([P, H, DH])
                        last = nc.tensor.matmul(psQ[:, h, :], ident_r[:, :], m, start=False, stop=True,
                                                skip_group_check=True)
                    last.then_inc(q_shift, 1)

                def tr_c(b, before):
                    for h in range(2):
                        free_T(before, h)
                        for n in range(4):
                            w = (4 * h + n) * P
                            last = nc.tensor.transpose(psT[:, h, n * P:n * P + P], ctx_in[:, w:w + P], ident[:, :])
                        last.then_inc(c_T, 1)

                def tr_k(b, j, before):
                    pe.wait_ge(k_exp, 4 * b + j + 1)
                    for h in range(2):
                        free_T(before, h)
                        for n in range(4):
                            w = (4 * h + n) * P
                            last = nc.tensor.transpose(psT[:, h, n * P:n * P + P], ek[:, j % 2, w:w + P], ident[:, :])
                        last.then_inc(k_T, 1)

                def tr_q(b, p, before):
                    pe.wait_ge(q_norm, 4 * b + p + 1)
                    for h in range(2):
                        free_T(before, h)
                        for j in range(CH):
                            w = h * HD + j * P
                            last = nc.tensor.transpose(psT[:, h, j * P:j * P + P], qe[:, p, w:w + P], ident[:, :])
                        last.then_inc(q_T, 1)

                def context(b, half):
                    if half == 0:
                        pe.wait_ge(k_lo, 8 * b + 8)
                        pe.wait_ge(c_lo, 2 * b + 2)
                        if started(b):
                            pe.wait_ge(o_out, 2 * b)
                        else:
                            pe.wait_ge(fold_lo, 2)
                    for n in range(BK // 2 * half, BK // 2 * (half + 1)):
                        last = three_pass(psX[:, 0, :], cT[0][:, n, :], cT[1][:, n, :], ekT[0][:, n, :],
                                          ekT[1][:, n, :], n == 0, n == BK - 1)
                    if half == 1:
                        last.then_inc(kc_mm, 1)

                def fold(b):
                    pe.wait_ge(kc_lo, b + 1)
                    if started(b):
                        pe.wait_ge(ss_read, b)
                    for j in range(CH):
                        w = slice(P * j, P * j + P)
                        last = three_pass(psX[:, j // 2, (j % 2) * 2 * P:(j % 2) * 2 * P + 2 * P],
                                          kc[0][:, w], kc[1][:, w], wvo[0][:, j, :], wvo[1][:, j, :], True, True)
                    last.then_inc(m_mm, 1)

                def output(b, h, chunks):
                    if h == 0:
                        pe.wait_ge(m_lo, b + 1)
                    if chunks[0] == 0:
                        pe.wait_ge(q_lo, 8 * b + 4 * h + 4)
                    v = slice(512 * h, 512 * h + 512)
                    for j in chunks:
                        last = three_pass(psX[:, h, :], mts[0][:, j, :], mts[1][:, j, :], qT[0][:, j, v],
                                          qT[1][:, j, v], j == 0, j == CH - 1)
                    if chunks[-1] == CH - 1:
                        last.then_inc(o_mm, 1)

                def square_norms(b):
                    pe.wait_ge(ones_ready, 1)
                    pe.wait_ge(o_sq, 2 * b + 2)
                    pe.wait_ge(o_out, 2 * b + 2)
                    for n in range(BK):
                        last = nc.tensor.matmul(psX[:, 1, n:n + 1], osq[:, n * P:n * P + P], ones[:, :],
                                                start=True, stop=True)
                    last.then_inc(ss_mm, 1)

                def spread_norms(b, before):
                    pe.wait_ge(root_step, NCH * (b + 4))
                    for h in range(2):
                        free_T(before, h)
                        for n in range(4):
                            dst = psT[:, h, n * P:n * P + P]
                            col = 4 * h + n
                            last = nc.tensor.matmul(dst, root_y[:, col:col + 1].broadcast_to([P, P]), ident[:, :],
                                                    start=True, stop=True)
                        last.then_inc(rn_mm, 1)

                def early_weights():
                    pe.wait_ge(k_exp, 4 * NB)
                    pe.wait_ge(q_exp, 4 * NB)
                    for t in range(EARLY):
                        pe.wait_ge(st_loaded[t], 16)
                        for h in range(2):
                            for n in range(4):
                                last = nc.tensor.transpose(ps[:, 2 * t + h, n * P:n * P + P],
                                                           stage[:, t, (4 * h + n) * P:(4 * h + n + 1) * P],
                                                           ident[:, :])
                            last.then_inc(w_T, 1)

                def body(b, head, tail, late, ahead):
                    order = ([("r", b - 2, 0)] * late + [("c", b, 0)] * head + [("q", b - 1, 1)] * tail
                             + [("k", b, 0)] * head + [("q", b - 1, 2)] * tail + [("k", b, 1)] * head
                             + [("q", b - 1, 3)] * tail + [("k", b, 2), ("q", b, 0), ("k", b, 3)] * head)
                    first = ("k", b - 1, 3) if tail else ("q", b - 2, 3) if late else None
                    before = [first] + order[:-1]
                    turn = iter(before)

                    if tail:
                        context(b - 1, 0)
                    if head:
                        if not started(b):
                            pe.wait_ge(w_lo, 2)
                            tr_c(b, next(turn))
                            transpose_wo()
                        mm_q(b, 0)
                    if late and not tail:
                        early_weights()
                    if late:
                        spread_norms(b - 2, next(turn))
                    if tail:
                        context(b - 1, 1)
                    if head:
                        if started(b):
                            tr_c(b, next(turn))
                        mm_k(b, 1)
                        shift_q(b, 0)
                    if tail and head:
                        fold(b - 1)
                    if tail:
                        tr_q(b - 1, 1, next(turn))
                    if tail and not head:
                        fold(b - 1)
                    if head:
                        mm_q(b, 1)
                        mm_k(b, 2)
                        tr_k(b, 0, next(turn))
                    if tail and head:
                        output(b - 1, 0, range(CH // 2))
                    if head:
                        shift_q(b, 1)
                        if not started(b):
                            fold_weights()
                    if tail:
                        tr_q(b - 1, 2, next(turn))
                    if head:
                        mm_k(b, 3)
                        mm_q(b, 2)
                        tr_k(b, 1, next(turn))
                    if tail and head:
                        output(b - 1, 0, range(CH // 2, CH))
                    if head:
                        shift_q(b, 2)
                    if tail:
                        tr_q(b - 1, 3, next(turn))
                    if ahead:
                        mm_k(b + 1, 0)
                    if head:
                        tr_k(b, 2, next(turn))
                    if tail:
                        if not head:
                            output(b - 1, 0, range(CH))
                        output(b - 1, 1, range(CH))
                    if head:
                        if not started(b):
                            mm_q(b, 3)
                        tr_q(b, 0, next(turn))
                        if started(b):
                            mm_q(b, 3)
                        tr_k(b, 3, next(turn))
                    if tail:
                        square_norms(b - 1)
                    if head:
                        shift_q(b, 3)

                pe.wait_ge(w_lo, 1)
                mm_k(0, 0)
                run(pe, body)

        ffn_phase(nc, ident, gates, ps, stage, st_loaded, w_T, EARLY, x2_stored, x2_first, x2_loaded,
                  started, wait_apart, rsqrt_step, three_pass, A, B, Wr, x2_dram, out)


def load_weight_rows(sp, t, A, B, stage, st_loaded, b_ready, w_T):
    E, R, D = A.shape
    P = 128
    EC, KC, ND = P // R, E * R // P, D // P
    slots = len(st_loaded)
    if t >= slots:
        before = t - slots
        if before < KC:
            sp.wait_ge(w_T, 2 * before + 2)
        else:
            k = before - KC
            sp.wait_ge(b_ready[k % 2], k // 2 + 1)
    slot = stage[:, t % slots, :]
    if t < KC:
        sp.dma_start(slot, A.rearrange("(k e) r d -> k (e r) d", e=EC)[t]).then_inc(st_loaded[t % slots], 16)
    else:
        sp.dma_start(slot.rearrange("p (e w) -> p e w", e=EC),
                     B.rearrange("(k e) (p d) r -> k p e (d r)", e=EC, d=ND)[t - KC]
                     ).then_inc(st_loaded[t % slots], 16)


def ffn_phase(nc, ident, gates, ps, stage, st_loaded, w_T, early, x2_stored, x2_first, x2_loaded,
              started, wait_apart, rsqrt_step, three_pass, A, B, Wr, x2_dram, out):
    f32 = mybir.dt.float32
    f32r = mybir.dt.float32r
    ALU = mybir.AluOpType
    ACT = mybir.ActivationFunctionType
    AX = mybir.AxisListType
    NB, T, D = out.shape
    E, R = A.shape[0], A.shape[1]
    KR = E * R
    P = 128
    DC = D // P
    KC = KR // P
    EC = E // KC
    SCALING = 32.0 / R
    LN_EPS = 1e-5
    NCH = 2 + 3 * 3
    NEG = -3.0e38
    ND = D // P
    SLOTS = 4
    with ExitStack() as ph:
        def sb(name, shape, dt=f32):
            return ph.enter_context(nc.sbuf_tensor(name, shape, dt))

        def sem(name):
            return ph.enter_context(nc.semaphore(name))

        NSTG = len(st_loaded)
        b_stage = sb("b_stage", [P, 2, D])
        wr_stage = sb("wr_stage", [E, D])
        aT = [sb("aT_hi", [P, DC, KR], f32r), sb("aT_lo", [P, DC, KR], f32r)]
        bT = [sb("bT_hi", [P, KC, D], f32r), sb("bT_lo", [P, KC, D], f32r)]
        wrT = sb("wrT", [P, DC, E])
        gf = sb("gf", [P, 1])
        x2_second = sb("x2_second", [P, D])
        x2b = [x2_first[:, :], x2_second[:, :], stage[:, 0, :], stage[:, 1, :]]
        res = b_stage
        y = sb("y", [P, D])
        yf = sb("yf", [P, DC, T])
        yT = [sb("yT_hi", [P, DC, T], f32r), sb("yT_lo", [P, DC, T], f32r)]
        hg = sb("hg", [P, KR])
        hT = [sb("hT_hi", [P, KC, T], f32r), sb("hT_lo", [P, KC, T], f32r)]
        bn = sb("bn2", [P, 2, 6])
        mv = sb("mv2", [P, 2])
        s1, y1, t1 = sb("s1", [P, 1]), sb("y1", [P, 1]), sb("t1", [P, 1])
        nb1 = sb("nb1", [P, 1])
        sc = sb("sc", [P, E])
        top8 = sb("top8", [P, 2, 8])
        rest = sb("rest", [P, 2, E])
        neg_top = sb("neg_top", [P, 1])
        ex = sb("ex", [P, E])
        gsel = sb("gsel", [P, E])
        gsum = sb("gsum", [P, 1])
        grec = sb("grec", [P, 1])
        gate = sb("gate", [P, E])

        dve_turns = sem("dve2_turns")
        wr_loaded, wr_T, wr_done = sem("wr_loaded"), sem("wr_T"), sem("wr_done")
        w_hi, w_lo, gf_done = sem("w2_hi"), sem("w2_lo"), sem("gf_done")
        b_ready = [sem("b_ready0"), sem("b_ready1")]
        out_stored = [sem("out_stored0"), sem("out_stored1")]
        stats_step, newton_step, nb_done, y_done = (
            sem("stats2_step"), sem("newton2_step"), sem("nb2_done"), sem("y_done"))
        y_T, y_full, y_hi, y_lo = sem("y_T"), sem("y_full"), sem("y_hi"), sem("y_lo")
        sc_mm, top_step, sc_exp = sem("sc_mm"), sem("top_step"), sem("sc_exp")
        h_mm, hg_done, h_T, h_hi, h_lo = (
            sem("h_mm"), sem("hg_done"), sem("h_T"), sem("h_hi"), sem("h_lo"))
        f_mm, res_done = sem("f_mm"), sem("res_done")
        psH, psF, psY, psG, psS = ps[:, 0:2, :], ps[:, 2:4, :], ps[:, 4:6, :], ps[:, 6, :], ps[:, 7, 0:E]
        TOP = 11

        def bank_of(u):
            return u % 4 if u < 2 * KC else (6, 2, 3)[(u - 2 * KC) % 3]

        def weight_part(part, t, h):
            bank = ps[:, bank_of(2 * t + h), :]
            if t < KC:
                return (aT[part][:, 4 * h:4 * h + 4, t * P:t * P + P], bank.rearrange("p (n r) -> p n r", r=P))
            dst = bT[part][:, t - KC, :].rearrange("p (q d) -> p q d", d=ND)[:, :, 4 * h:4 * h + 4]
            return dst, bank.rearrange("p (n q) -> p q n", q=P)

        def reorder(copy, k):
            return copy(b_stage[:, k % 2, :].rearrange("p (d e r) -> p e d r", e=EC, d=ND),
                        stage[:, (KC + k) % NSTG, :].rearrange("p (e d r) -> p e d r", e=EC, d=ND)
                        ).then_inc(b_ready[k % 2], 1)

        block = ph.enter_context(nc.Block())

        @block.sync
        def _(sp):
            def load(b, slot):
                sp.dma_start(x2b[slot],
                             x2_dram[bass.ds(b, 1)].rearrange("o p n -> (o p) n")).then_inc(x2_loaded[slot], 16)

            for t in range(NSTG + early, 2 * KC):
                load_weight_rows(sp, t, A, B, stage, st_loaded, b_ready, w_T)
                if t == NSTG + 2:
                    sp.dma_start(wr_stage[:, :], Wr).then_inc(wr_loaded, 16)
                if t == KC + 1:
                    load(1, 1)
            sp.wait_ge(x2_stored, 16 * NB)
            for slot in (2, 3):
                k = KC - NSTG + slot - 2
                sp.wait_ge(b_ready[k % 2], k // 2 + 1)
                load(slot, slot)

            def group(i, last):
                for j in range(SLOTS):
                    b = SLOTS * i + j
                    sp.wait_ge(res_done, 2 * b + 2)
                    sp.dma_start(out[bass.ds(b, 1)].rearrange("o p n -> (o p) n"),
                                 res[:, j % 2, :]).then_inc(out_stored[j % 2], 16)
                    if not last:
                        load(b + SLOTS, j)

            with sp.Fori(0, NB // SLOTS - 1) as i:
                group(i, False)
            group(NB // SLOTS - 1, True)
            for half in range(2):
                sp.wait_ge(out_stored[half], 16 * (NB // 2))

        @block.gpsimd
        def _(pool):
            def lo_y(b):
                for h in range(2):
                    n = slice(4 * h, 4 * h + 4)
                    pool.wait_ge(y_hi, 2 * b + h + 1)
                    nc.gpsimd.tensor_tensor(yT[1][:, n, :], yf[:, n, :], yT[0][:, n, :].bitcast(f32),
                                            ALU.subtract).then_inc(y_lo, 1)

            t = KC + 1
            pool.wait_ge(st_loaded[t % NSTG], 16 * (t // NSTG + 1))
            reorder(nc.gpsimd.tensor_copy, 1)
            lo_y(0)
            with pool.Fori(1, NB) as b:
                lo_y(b)

        @block.tensor
        def _(pe):
            def weight(t):
                if t < KC:
                    pe.wait_ge(st_loaded[t % NSTG], 16 * (t // NSTG + 1))
                else:
                    k = t - KC
                    pe.wait_ge(b_ready[k % 2], k // 2 + 1)
                for h in range(2):
                    u = 2 * t + h
                    ahead = 4 if t < KC else 3
                    if u >= ahead and u != 2 * KC:
                        pe.wait_ge(w_lo, u - ahead + 1)
                    for n in range(4):
                        m = 4 * h + n
                        if t < KC:
                            src = stage[:, t % NSTG, m * P:m * P + P]
                        else:
                            src = b_stage[:, k % 2, m * P:m * P + P]
                        last = nc.tensor.transpose(ps[:, bank_of(u), n * P:n * P + P], src, ident[:, :])
                    last.then_inc(w_T, 1)

            def tr_y(b):
                pe.wait_ge(y_done, b + 1)
                for h in range(2):
                    if started(b):
                        pe.wait_ge(y_full, 2 * b - 2 + h + 1)
                    for n in range(4):
                        w = (4 * h + n) * P
                        last = nc.tensor.transpose(psY[:, h, n * P:n * P + P], y[:, w:w + P], ident[:, :])
                    last.then_inc(y_T, 1)

            def scores(b):
                pe.wait_ge(y_full, 2 * b + 2)
                if started(b):
                    pe.wait_ge(top_step, TOP * (b - 1) + 1)
                for m in range(DC):
                    last = nc.tensor.matmul(psS, yf[:, m, :], wrT[:, m, :], start=m == 0, stop=m == DC - 1)
                last.then_inc(sc_mm, 1)

            def up(b, g, chunks):
                if g == 0 and chunks[0] == 0:
                    pe.wait_ge(y_lo, 2 * b + 2)
                if started(b):
                    pe.wait_ge(hg_done, 2 * b - 2 + g + 1)
                v = slice(512 * g, 512 * g + 512)
                for m in chunks:
                    last = three_pass(psH[:, g, :], yT[0][:, m, :], yT[1][:, m, :], aT[0][:, m, v], aT[1][:, m, v],
                                      m == 0, m == DC - 1)
                if chunks[-1] == DC - 1:
                    last.then_inc(h_mm, 1)

            def tr_h(b, g):
                pe.wait_ge(hg_done, 2 * b + g + 1)
                if g == 1 or started(b):
                    pe.wait_ge(h_lo, 2 * b + g)
                else:
                    pe.wait_ge(w_lo, 4 * KC)
                for n in range(4):
                    w = (4 * g + n) * P
                    last = nc.tensor.transpose(psG[:, n * P:n * P + P], hg[:, w:w + P], ident[:, :])
                last.then_inc(h_T, 1)

            def down(b):
                for part in range(2):
                    pe.wait_ge(h_lo, 2 * b + part + 1)
                    for g in range(2):
                        if part == 0 and started(b):
                            pe.wait_ge(res_done, 2 * b - 2 + g + 1)
                        v = slice(512 * g, 512 * g + 512)
                        for m in range(KC // 2 * part, KC // 2 * (part + 1)):
                            last = three_pass(psF[:, g, :], hT[0][:, m, :], hT[1][:, m, :], bT[0][:, m, v],
                                              bT[1][:, m, v], m == 0, m == KC - 1)
                        if part == 1:
                            last.then_inc(f_mm, 1)

            def body(b, nxt):
                if started(b):
                    up(b, 0, range(DC))
                if nxt:
                    tr_y(b + 1)
                tr_h(b, 0)
                if started(b):
                    up(b, 1, range(DC))
                if nxt:
                    scores(b + 1)
                tr_h(b, 1)
                down(b)

            for t in range(early, KC):
                weight(t)
            pe.wait_ge(wr_loaded, 16)
            for m in range(DC):
                last = nc.tensor.transpose(ps[:, 7, m * E:m * E + E], wr_stage[:, m * P:m * P + P], ident[0:E, 0:E])
            last.then_inc(wr_T, 1)
            weight(KC)
            tr_y(0)
            weight(KC + 1)
            pe.wait_ge(wr_done, 1)
            scores(0)
            done = 0
            for k in range(2, KC):
                weight(KC + k)
                until = 2 * DC * (k - 1) // (KC - 2)
                for u in range(done, until):
                    up(0, u // DC, [u % DC])
                done = until
            body(0, True)
            with pe.Fori(1, NB - 1) as b:
                body(b, True)
            body(NB - 1, False)

        @block.scalar
        def _(act):
            nc.scalar.activation(gf[:, :], gates[:, 1:2], ACT.Copy, scale=SCALING).then_inc(gf_done, 1)

            def hi_weight(t):
                for h in range(2):
                    act.wait_ge(w_T, 2 * t + h + 1)
                    dst, src = weight_part(0, t, h)
                    nc.scalar.activation(dst, src, ACT.Copy).then_inc(w_hi, 1)

            def normalise(b, slot):
                act.wait_ge(nb_done, b + 1)
                if started(b):
                    act.wait_ge(y_T, 2 * b)
                nc.scalar.activation(y[:, :], x2b[slot], ACT.Identity, bias=nb1[:, 0:1],
                                     scale=y1[:, 0:1]).then_inc(y_done, 1)

            def full_y(b):
                if started(b):
                    act.wait_ge(sc_mm, b)
                    act.wait_ge(y_lo, 2 * b)
                for h in range(2):
                    act.wait_ge(y_T, 2 * b + h + 1)
                    nc.scalar.activation(yf[:, 4 * h:4 * h + 4, :],
                                         psY[:, h, :].rearrange("p (n c) -> p n c", c=P),
                                         ACT.Copy).then_inc(y_full, 1)

            def hi_y(b):
                act.wait_ge(y_full, 2 * b + 2)
                if started(b):
                    act.wait_ge(h_mm, 2 * b)
                for h in range(2):
                    n = slice(4 * h, 4 * h + 4)
                    nc.scalar.activation(yT[0][:, n, :], yf[:, n, :], ACT.Copy).then_inc(y_hi, 1)

            def hi_h(b, g):
                act.wait_ge(h_T, 2 * b + g + 1)
                nc.scalar.activation(hT[0][:, 4 * g:4 * g + 4, :], psG.rearrange("p (n c) -> p n c", c=P),
                                     ACT.Copy).then_inc(h_hi, 1)

            def exp_scores(b):
                act.wait_ge(top_step, TOP * b + 3)
                nc.scalar.activation(ex[:, :], sc[:, :], ACT.Exp, bias=neg_top[:, 0:1]).then_inc(sc_exp, 1)

            def body(b, slot, nxt, nxt2):
                if nxt:
                    full_y(b + 1)
                hi_h(b, 0)
                hi_h(b, 1)
                if nxt:
                    hi_y(b + 1)
                    exp_scores(b + 1)
                if nxt2:
                    normalise(b + 2, (slot + 2) % SLOTS)

            for t in range(KC):
                hi_weight(t)
            act.wait_ge(wr_T, 1)
            nc.scalar.activation(wrT[:, :, :].rearrange("p a b -> p (a b)"), ps[:, 7, :],
                                 ACT.Copy).then_inc(wr_done, 1)
            normalise(0, 0)
            hi_weight(KC)
            full_y(0)
            hi_y(0)
            for k in range(1, KC):
                hi_weight(KC + k)
                if k == 4:
                    exp_scores(0)
            normalise(1, 1)
            for b in range(SLOTS):
                body(b, b, True, True)
            with act.Fori(1, NB // SLOTS - 1) as i:
                for j in range(SLOTS):
                    body(SLOTS * i + j, j, True, True)
            for j in range(SLOTS):
                body(NB - SLOTS + j, j, j < SLOTS - 1, j < SLOTS - 2)

        @block.vector
        def _(dve):
            def lo_weight(t, h):
                dve.wait_ge(w_hi, 2 * t + h + 1)
                dst, src = weight_part(1, t, h)
                hi, _ = weight_part(0, t, h)
                nc.vector.tensor_tensor(dst, src, hi.bitcast(f32), ALU.subtract).then_inc(w_lo, 1)

            def reorder_rows(k):
                t = KC + k
                dve.wait_ge(st_loaded[t % NSTG], 16 * (t // NSTG + 1))
                if k >= 2:
                    dve.wait_ge(w_T, 2 * (t - 2) + 2)
                reorder(nc.vector.tensor_copy, k)

            NS = 4

            def stats_step_of(b, slot, uses, k):
                if k == 0:
                    dve.wait_ge(x2_loaded[slot], 16 * (uses + 1))
                    for h in range(2):
                        nc.vector.bn_stats(bn[:, h, :], x2b[slot][:, 512 * h:512 * h + 512]).then_inc(stats_step, 1)
                elif k == 1:
                    wait_apart(dve, dve_turns, (stats_step, NS * b + 2), *([(y_done, b)] if started(b) else []))
                    nc.vector.bn_aggr(mv[:, :], bn[:, :, :].rearrange("p a b -> p (a b)")).then_inc(stats_step, 1)
                elif k == 2:
                    dve.wait_ge(stats_step, NS * b + 3)
                    nc.vector.tensor_scalar(s1[:, :], mv[:, 1:2], LN_EPS, None, ALU.add).then_inc(stats_step, 1)
                elif k < STEPS - 1:
                    if k == 3:
                        dve.wait_ge(stats_step, NS * b + 4)
                    rsqrt_step(dve, k - 3, y1[:, :], t1[:, :], s1[:, :], newton_step, NCH * b)
                else:
                    dve.wait_ge(newton_step, NCH * (b + 1))
                    nc.vector.scalar_tensor_tensor(nb1[:, :], mv[:, 0:1], -1.0, y1[:, :], ALU.mult,
                                                   ALU.mult).then_inc(nb_done, 1)

            STEPS = NCH + 4

            def stats(b, slot, uses):
                for k in range(STEPS):
                    stats_step_of(b, slot, uses, k)

            def route_step(b, k):
                before = (top_step, TOP * b + k)
                if k == 0:
                    dve.wait_ge(sc_mm, b + 1)
                    last = nc.vector.tensor_copy(sc[:, :], psS)
                elif k == 1:
                    wait_apart(dve, dve_turns, before)
                    last = nc.vector.max(top8[:, 0, :], sc[:, :])
                elif k == 2:
                    dve.wait_ge(*before)
                    last = nc.vector.tensor_scalar(neg_top[:, :], top8[:, 0, 0:1], -1.0, None, ALU.mult)
                elif k == 3:
                    wait_apart(dve, dve_turns, before)
                    last = nc.vector.match_replace(rest[:, 0, :], top8[:, 0, :], sc[:, :], NEG)
                elif k == 4:
                    wait_apart(dve, dve_turns, before)
                    last = nc.vector.max(top8[:, 1, :], rest[:, 0, :])
                elif k == 5:
                    wait_apart(dve, dve_turns, before)
                    last = nc.vector.match_replace(rest[:, 1, :], top8[:, 1, :], rest[:, 0, :], NEG)
                elif k == 6:
                    dve.wait_ge(*before)
                    last = nc.vector.tensor_tensor(gsel[:, :], sc[:, :], rest[:, 1, :], ALU.not_equal)
                elif k == 7:
                    dve.wait_ge(*before)
                    dve.wait_ge(sc_exp, b + 1)
                    last = nc.vector.tensor_tensor(gsel[:, :], gsel[:, :], ex[:, :], ALU.mult)
                elif k == 8:
                    dve.wait_ge(*before)
                    last = nc.vector.tensor_reduce(gsum[:, :], gsel[:, :], axis=AX.X, op=ALU.add)
                elif k == 9:
                    dve.wait_ge(*before)
                    last = nc.vector.reciprocal(grec[:, :], gsum[:, :])
                else:
                    dve.wait_ge(*before)
                    last = nc.vector.tensor_scalar(gate[:, :], gsel[:, :], grec[:, 0:1], None, ALU.mult)
                last.then_inc(top_step, 1)

            def route(b):
                for k in range(TOP):
                    route_step(b, k)

            def gated(b, g):
                dve.wait_ge(top_step, TOP * (b + 1))
                dve.wait_ge(h_mm, 2 * b + g + 1)
                if started(b):
                    dve.wait_ge(h_T, 2 * b - 1 + g)
                n = 512 // R
                nc.vector.tensor_tensor(hg[:, 512 * g:512 * g + 512].rearrange("p (e r) -> p e r", r=R),
                                        psH[:, g, :].rearrange("p (e r) -> p e r", r=R),
                                        gate[:, n * g:n * g + n].unsqueeze(2).broadcast_to([P, n, R]),
                                        ALU.mult).then_inc(hg_done, 1)

            def lo_h(b, g):
                dve.wait_ge(h_hi, 2 * b + g + 1)
                nc.vector.tensor_tensor(hT[1][:, 4 * g:4 * g + 4, :], psG.rearrange("p (n c) -> p n c", c=P),
                                        hT[0][:, 4 * g:4 * g + 4, :].bitcast(f32),
                                        ALU.subtract).then_inc(h_lo, 1)

            def result(b, slot, stores):
                for g in range(2):
                    dve.wait_ge(f_mm, 2 * b + g + 1)
                    if g == 0 and started(stores):
                        dve.wait_ge(out_stored[slot % 2], 16 * stores)
                    v = slice(512 * g, 512 * g + 512)
                    nc.vector.scalar_tensor_tensor(res[:, slot % 2, v], psF[:, g, :], gf[:, 0:1], x2b[slot][:, v],
                                                   ALU.mult, ALU.add).then_inc(res_done, 1)

            def body(i, slot, nxt, nxt2):
                b = SLOTS * i + slot
                gated(b, 0)
                lo_h(b, 0)
                if nxt2 and started(b):
                    stats(b + 2, (slot + 2) % SLOTS, i + (slot + 2) // SLOTS)
                gated(b, 1)
                lo_h(b, 1)
                if not started(b):
                    stats(b + 2, 2, 0)
                if nxt:
                    route(b + 1)
                result(b, slot, 2 * i + slot // 2)

            dve.wait_ge(gf_done, 1)
            for t in range(KC):
                for h in range(2):
                    lo_weight(t, h)
                    if 2 * t + h < STEPS:
                        stats_step_of(0, 0, 0, 2 * t + h)
                if t == KC - 2:
                    reorder_rows(0)
            for k in range(KC):
                if 0 < k < KC - 1:
                    reorder_rows(k + 1)
                for h in range(2):
                    u = 2 * k + h
                    lo_weight(KC + k, h)
                    if u < STEPS:
                        stats_step_of(1, 1, 0, u)
                    if 4 <= u < 4 + TOP:
                        route_step(0, u - 4)
            for j in range(SLOTS):
                body(0, j, True, True)
            with dve.Fori(1, NB // SLOTS - 1) as i:
                for j in range(SLOTS):
                    body(i, j, True, True)
            for j in range(SLOTS):
                body(NB // SLOTS - 1, j, j < SLOTS - 1, j < SLOTS - 2)


_INS = ["x", "ctx_4096", "g_xattn", "g_ffn", "L0_xattn_Wq", "L0_xattn_Wk", "L0_xattn_Wv", "L0_xattn_Wo",
        "L0_xattn_bo", "L0_xattn_g", "L0_ffn_A", "L0_ffn_B", "L0_ffn_Wr"]


def kernel(**inputs):
    import numpy as _np
    import concourse.bacc as _bacc
    from concourse import mybir as _mybir
    from concourse.bass_utils import run_bass_kernel_spmd as _run

    nc = _bacc.Bacc("TRN2", target_bir_lowering=False, num_devices=1)
    arrays, args = {}, []
    for name in _INS:
        a = _np.ascontiguousarray(inputs[name])
        arrays[f"in_{name}"] = a
        args.append(nc.dram_tensor(f"in_{name}", a.shape, _mybir.dt.from_np(a.dtype), kind="ExternalInput").ap())
    shape = tuple(inputs["x"].shape)
    scratch = nc.dram_tensor("x2_scratch", shape, _mybir.dt.float32, kind="Internal").ap()
    out = nc.dram_tensor("out_0", shape, _mybir.dt.float32, kind="ExternalOutput").ap()
    flamingo_layer(nc, *args, scratch, out)
    r = _run(nc, [arrays], core_ids=[0])
    return r.results[0]["out_0"]
```
